# Optimizing a Trainium2 kernel written in Bass

```python
import numpy as np
import jax
import jax.numpy as jnp

def _softmax(x, axis=-1):
    return jax.nn.softmax(x, axis=axis)

def _gelu(x):
    return jax.nn.gelu(x, approximate=True)

def _silu(x):
    return jax.nn.silu(x)

def _sigmoid(x):
    return jax.nn.sigmoid(x)

def _layernorm(x, axis=-1, eps=1e-05):
    m = jnp.mean(x, axis=axis, keepdims=True)
    v = jnp.var(x, axis=axis, keepdims=True)
    return (x - m) / jnp.sqrt(v + eps)

def _scatter_add(tgt, idx, src, axis=0):
    return tgt.at[idx].add(src)

def _segment_sum(src, seg, n):
    return jax.ops.segment_sum(src, seg, n)
kernel_name = 'mk_conv_preact_d1_conv_nchw64_r2_faa51e'

def setup_inputs(seed: int=0):
    np.random.seed(seed)
    _w = jnp.asarray

    def _rec_inputs():
        import jax
        import jax.numpy as jnp
        _gk = jax.random.key(seed)
        x = 7.22e-05 + 1 * jax.random.normal(jax.random.fold_in(_gk, 1), (32, 32, 32, 32), jnp.float32)
        return x
    x = _rec_inputs()

    def _L0_conv_setup():
        import jax, jax.numpy as jnp
        import numpy as np
        PS = 8
        E = 8

        def patchify(x, ps):
            B, C, h, w = x.shape
            nv, nh = (h // ps, w // ps)
            xp = jnp.pad(x, ((0, 0), (0, 0), (1, 1), (1, 1)))
            k = ps + 2
            iv = jnp.arange(nv)[:, None] * ps + jnp.arange(k)[None, :]
            ih = jnp.arange(nh)[:, None] * ps + jnp.arange(k)[None, :]
            win = xp[:, :, iv[:, None, :, None], ih[None, :, None, :]]
            return win.reshape(B * nv * nh, C, k, k)

        def unpatchify(y, h, w, ps):
            y = y[:, :, 1:-1, 1:-1]
            nv, nh = (h // ps, w // ps)
            C = y.shape[1]
            p = y.reshape(-1, C, nv * nh, ps * ps)
            B = p.shape[0]
            p = p.transpose(0, 1, 3, 2)
            p = p.reshape(B, C, ps, ps, nv, nh)
            p = p.transpose(0, 1, 4, 2, 5, 3)
            return p.reshape(B, C, h, w)
        key = jax.random.key(seed)
        k1, k2, k3 = jax.random.split(key, 3)
        C = 32
        x = jax.random.normal(k1, (32, C, 32, 32), dtype=jnp.float32)
        Wg = jax.random.normal(k2, (C, E), dtype=jnp.float32) * 0.05
        bg = jnp.zeros((E,), dtype=jnp.float32)
        Wexp = jax.random.normal(k3, (E, C, C, 3, 3), dtype=jnp.float32) * 0.05
        bexp = jnp.zeros((E, C), dtype=jnp.float32)
        return {'x': x, 'Wg': Wg, 'bg': bg, 'Wexp': Wexp, 'bexp': bexp}
    _L0_conv_all = _L0_conv_setup()
    _L0_conv_in = {k: v for k, v in _L0_conv_all.items() if k in ('Wg', 'bg', 'Wexp', 'bexp')}
    del _L0_conv_all
    return {'x': x, 'L0_conv_Wg': _L0_conv_in['Wg'], 'L0_conv_bg': _L0_conv_in['bg'], 'L0_conv_Wexp': _L0_conv_in['Wexp'], 'L0_conv_bexp': _L0_conv_in['bexp']}

def reference(x, L0_conv_Wg, L0_conv_bg, L0_conv_Wexp, L0_conv_bexp):
    import jax
    import jax.numpy as jnp

    def _L0_conv_ref(x, Wg, bg, Wexp, bexp):
        import jax, jax.numpy as jnp
        import numpy as np
        PS = 8
        E = 8

        def patchify(x, ps):
            B, C, h, w = x.shape
            nv, nh = (h // ps, w // ps)
            xp = jnp.pad(x, ((0, 0), (0, 0), (1, 1), (1, 1)))
            k = ps + 2
            iv = jnp.arange(nv)[:, None] * ps + jnp.arange(k)[None, :]
            ih = jnp.arange(nh)[:, None] * ps + jnp.arange(k)[None, :]
            win = xp[:, :, iv[:, None, :, None], ih[None, :, None, :]]
            return win.reshape(B * nv * nh, C, k, k)

        def unpatchify(y, h, w, ps):
            y = y[:, :, 1:-1, 1:-1]
            nv, nh = (h // ps, w // ps)
            C = y.shape[1]
            p = y.reshape(-1, C, nv * nh, ps * ps)
            B = p.shape[0]
            p = p.transpose(0, 1, 3, 2)
            p = p.reshape(B, C, ps, ps, nv, nh)
            p = p.transpose(0, 1, 4, 2, 5, 3)
            return p.reshape(B, C, h, w)
        B, C, H, W = x.shape
        v_pad = PS - H % PS
        h_pad = PS - W % PS
        x = jnp.pad(x, ((0, 0), (0, 0), (0, v_pad), (0, h_pad)))
        h, w = (x.shape[2], x.shape[3])
        patched = patchify(x, PS)
        feat = patched.mean(axis=(2, 3))
        logits = feat @ Wg + bg
        probs = jax.nn.softmax(logits, axis=-1)
        routing = jax.nn.one_hot(jnp.argmax(logits, axis=-1), E, dtype=probs.dtype) * probs

        def expert(w_, b_):
            y = jax.lax.conv_general_dilated(patched, w_, (1, 1), 'SAME', dimension_numbers=('NCHW', 'OIHW', 'NCHW'))
            return jax.nn.relu(y + b_[None, :, None, None])
        outs = jax.vmap(expert)(Wexp, bexp)
        combined = jnp.einsum('ne,encij->ncij', routing, outs)
        y = unpatchify(combined, h, w, PS)
        return y[:, :, :H, :W]

    def _gn(v, G=32, eps=1e-05):
        B_, C_, H_, W_ = v.shape
        g = v.reshape(B_, G, C_ // G, H_, W_)
        m = jnp.mean(g, axis=(2, 3, 4), keepdims=True)
        s = jnp.var(g, axis=(2, 3, 4), keepdims=True)
        return ((g - m) / jnp.sqrt(s + eps)).reshape(v.shape)

    def _ln_c(v, eps=1e-06):
        m = jnp.mean(v, axis=1, keepdims=True)
        s = jnp.var(v, axis=1, keepdims=True)
        return (v - m) / jnp.sqrt(s + eps)

    def _ln_t(v, eps=1e-05):
        m = jnp.mean(v, axis=-1, keepdims=True)
        s = jnp.var(v, axis=-1, keepdims=True)
        return (v - m) / jnp.sqrt(s + eps)

    def _to_tokens(v):
        B_, C_, H_, W_ = v.shape
        return v.reshape(B_, C_, H_ * W_).transpose(0, 2, 1)

    def _from_tokens(t, like):
        B_, C_, H_, W_ = like.shape
        return t.transpose(0, 2, 1).reshape(B_, C_, H_, W_)
    x = x + _L0_conv_ref(_gn(x), L0_conv_Wg, L0_conv_bg, L0_conv_Wexp, L0_conv_bexp)
    return x

_drawn_inputs = setup_inputs


def setup_inputs(seed=0):
    import zlib

    import numpy as np

    out = dict(_drawn_inputs(seed))
    spreads = {'L0_conv_bg': (0.0, 0.1), 'L0_conv_bexp': (0.0, 0.8)}
    factors = {}
    for name, (base, spread) in spreads.items():
        noise = np.random.default_rng([zlib.crc32(name.encode()), seed]).standard_normal(out[name].shape)
        drawn = base * np.exp(spread * noise) if base else spread * noise
        out[name] = jnp.asarray(drawn.astype(out[name].dtype))
    for name, factor in factors.items():
        out[name] = (out[name] * factor).astype(out[name].dtype)
    return out
```

```python
from contextlib import ExitStack

import concourse.bass as bass
from concourse import mybir

B, C, H, W = 32, 32, 32, 32
E, TAPS, PS = 8, 3, 8
NB = 5
NP = NB * NB
GI, GROUPS = 4, B // 4
GN = GI * NP
PIX = PS * PS
WIN = PS + 2
PITCH = NB * PS + 2
KROWS = PS * WIN
KC = TAPS * C + 1
NW = TAPS * C
WG = C // 16
PARTS = 3
LOT, LOTS = NB, NP // NB
CH = 5
CHUNKS = [(t, min(CH, NW - t)) for t in range(0, NW, CH)]

C_ID, C_OWN, C_PATCH, C_CODE, C_END = 0, 128, 256, 256 + NP, 384 + NP


def group_order(has_next):
    chunks = [("chunk", c) for c in range(len(CHUNKS))] if has_next else []
    order = []
    for n in range(NP):
        order.append(("conv", n))
        if has_next and n in (9, 11, 14):
            order.append(({9: "turn", 11: "logits", 14: "select"}[n],))
        if n >= 15 and chunks:
            order.append(chunks.pop(0))
        if n >= 20 and chunks:
            order.append(chunks.pop(0))
        if n >= LOT and n % LOT == 2:
            order.append(("blocks", n // LOT - 1))
    order.append(("blocks", LOTS - 1))
    order += chunks
    return order + [("channels", 0), ("channels", 1)]


def build(nc, x, wg, bg, wexp, bexp, consts, out):
    fp32, bf16 = mybir.dt.float32, mybir.dt.bfloat16
    ALU, ACT, AX = mybir.AluOpType, mybir.ActivationFunctionType, mybir.AxisListType

    with ExitStack() as ctx:
        def sb(name, shape, dt=fp32):
            return ctx.enter_context(nc.sbuf_tensor(name, shape, dt))

        def bank(name, banks=1):
            return ctx.enter_context(nc.psum_tensor(name, [128, 512 * banks], fp32))

        def sem(name):
            return ctx.enter_context(nc.semaphore(name))

        XG = [sb(f"XG{u}", [128, GN, KROWS]) for u in range(2)]
        WS = [sb(f"WS{u}", [128, GN, NW]) for u in range(2)]
        XC = sb("XC", [128, H * W])
        XR = [sb(f"XR{u}", [128, GI, 256]) for u in range(2)]
        XN = sb("XN", [128, PITCH * PITCH])
        WY = sb("WY", [128, GI * NP * C])
        Z = [sb(f"Z{i}", [128, LOT, PIX]) for i in range(2)]
        KEPT = sb("KEPT", [64, GI, 4, C * 4])
        WP = sb("WP", [128, C, TAPS, KC], bf16)
        BT = sb("BT", [128, WG])
        CONST = sb("CONST", [128, C_END])
        IDB = sb("IDB", [128, 128], bf16)
        WGT = sb("WGT", [C, E])
        BG = sb("BG", [128, E])
        STATS = sb("STATS", [128, GROUPS, 12])
        MV = sb("MV", [128, GROUPS, 2])
        VAR, ROOT, RSTD, NEWT = (sb(n, [128, GROUPS]) for n in ("VAR", "ROOT", "RSTD", "NEWT"))
        SUMS = sb("SUMS", [128, NP])
        FEAT = sb("FEAT", [128, C])
        FEATT = sb("FEATT", [C, GN])
        LOGIT, LMINUS, LEXP, LCODE = (sb(n, [128, E]) for n in ("LOGIT", "LMINUS", "LEXP", "LCODE"))
        LMAX, LSUM, LPICK, PROB = (sb(n, [128, 1]) for n in ("LMAX", "LSUM", "LPICK", "PROB"))
        HOT = sb("HOT", [128, 128], bf16)
        PSEL = sb("PSEL", [128, NP])
        HOTT = sb("HOTT", [128, GN], bf16)
        PB = [sb(f"PB{u}", [128, NP]) for u in range(2)]

        XALL = WS[1][:].rearrange("p n w -> p (n w)")[:, 0:GROUPS * H * W].rearrange("p (g f) -> p g f", g=GROUPS)
        Y = WY[0:PIX].rearrange("p (b f) -> p b f", b=GI)
        ident = CONST[:, C_ID:C_ID + 128]

        WROW = WG * TAPS * KC
        spare = XG[1][:].rearrange("p n k -> p (n k)")
        WR = spare[:, 0:WG * C * 9]
        W0 = spare[:, 1024:1024 + WROW]
        WPART = spare[:, 2048:2048 + PARTS * WROW // 2].bitcast(bf16).rearrange("p (t f) -> p t f", t=PARTS)

        conv_bank = [bank(f"conv_bank{i}") for i in range(2)]
        chunk_bank = [bank(f"chunk_bank{i}") for i in range(2)]
        channels_bank = [bank(f"channels_bank{i}") for i in range(2)]
        blocks_bank = bank("blocks_bank", 2)

        parts_dram = nc.dram_tensor("weight_parts", (PARTS, 128, WROW), bf16).ap()
        windows_dram = [nc.dram_tensor(f"windows{u}", (GI * C * NP, WIN * WIN), fp32).ap() for u in range(2)]
        sums_dram = nc.dram_tensor("sums", (GI * C, NP), fp32).ap()

        x_loaded = [sem(f"x_loaded{g}") for g in range(GROUPS)]
        xc_loaded = sem("xc_loaded")
        w_loaded, bias_loaded, small_loaded = sem("w_loaded"), sem("bias_loaded"), sem("small_loaded")
        parts_split, parts_written, wp_loaded = sem("parts_split"), sem("parts_written"), sem("wp_loaded")
        pads_set = sem("pads_set")
        chain = sem("chain")
        var_ready, root_ready, normalised = sem("var_ready"), sem("root_ready"), sem("normalised")
        windows_ready, windows_written = sem("windows_ready"), sem("windows_written")
        sums_ready, sums_written, feat_loaded = sem("sums_ready"), sem("sums_written"), sem("feat_loaded")
        xg_loaded = [sem(f"xg_loaded{u}") for u in range(2)]
        residual_loaded = [sem(f"residual_loaded{u}") for u in range(2)]
        turned, feat_ready, logits_done = sem("turned"), sem("feat_ready"), sem("logits_done")
        centred, exp_done = sem("centred"), sem("exp_done")
        onehot_ready, select_done, select_copied = sem("onehot_ready"), sem("select_done"), sem("select_copied")
        chunk_done, chunk_copied = sem("chunk_done"), sem("chunk_copied")
        conv_done, z_ready = sem("conv_done"), sem("z_ready")
        blocks_done, blocks_copied = sem("blocks_done"), sem("blocks_copied")
        pool_go, pe_go, kept_ready = sem("pool_go"), sem("pe_go"), sem("kept_ready")
        channels_done, out_ready, out_stored = sem("channels_done"), sem("out_ready"), sem("out_stored")

        NCH = len(CHUNKS)
        x_rows = x.rearrange("(g b) c h w -> g (b c) (h w)", b=GI)
        x_rows_all = x.rearrange("b c h w -> (b c) (h w)")
        x_quarters = x.rearrange("b c (v r) w -> (c v) b (r w)", v=4)
        out_quarters = out.rearrange("b c (v r) w -> (c v) b (r w)", v=4)

        block = ctx.enter_context(nc.Block())

        @block.sync
        def _(sp):
            sp.dma_start(WR, wexp.rearrange("e (g c) i h w -> (e g) (c i h w)", c=WG)).then_inc(w_loaded, 16)
            sp.dma_start(BT[:], bexp.rearrange("e (g c) -> (e g) c", c=WG)).then_inc(bias_loaded, 16)
            for g in range(GROUPS):
                sp.dma_start(XALL[:, g, :], x_rows[g]).then_inc(x_loaded[g], 16)
            sp.wait_ge(parts_split, 1)
            sp.dma_start(parts_dram.rearrange("t p f -> p t f"), WPART).then_inc(parts_written, 16)
            sp.wait_ge(parts_written, 16)
            sp.wait_ge(pads_set, 3)
            sp.dma_start(WP[0:PARTS * E].rearrange("p c k m -> p (c k m)"),
                         parts_dram.rearrange("t (e g) f -> (t e) (g f)", g=16)).then_inc(wp_loaded, 16)
            sp.dma_start(XC[:], x_rows[0]).then_inc(xc_loaded, 16)

            def patches(g, u):
                sp.wait_ge(windows_ready, g + 1)
                sp.dma_start(windows_dram[u].rearrange("(p k) w -> p (k w)", k=NP),
                             WY[:, 0:NP * WIN * WIN]).then_inc(windows_written, 16)
                sp.wait_ge(windows_written, g * 16 + 16)
                for ky in range(TAPS):
                    sp.dma_start(XG[u][ky * C:(ky + 1) * C],
                                 windows_dram[u].rearrange("(n j) w -> j n w", j=C)[:, :, ky * WIN:ky * WIN + KROWS]
                                 ).then_inc(xg_loaded[u], 16)

            def quarters(g, u):
                sp.dma_start(XR[u][:], x_quarters[:, bass.ds(g * GI, GI), :]).then_inc(residual_loaded[u], 16)

            sp.wait_ge(pads_set, 4)
            patches(0, 0)
            quarters(0, 0)

            def group(g, u, has_next, i):
                if has_next:
                    sp.wait_ge(normalised, g + 1)
                    sp.dma_start(XC[:], x_rows_all[bass.ds((g + 1) * GI * C, GI * C), :]).then_inc(xc_loaded, 16)
                    patches(g + 1, 1 - u)
                    sp.wait_ge(out_stored, g * 32 + 16)
                    quarters(g + 1, 1 - u)
                for q in range(2):
                    sp.wait_ge(out_ready, g * 2 + q + 1)
                    sp.dma_start(out_quarters[:, bass.ds(g * GI + 2 * q, 2), :],
                                 XR[u][:, 2 * q:2 * q + 2, :]).then_inc(out_stored, 16)

            sp.sem_inc(out_stored, 16)
            with sp.Fori(0, 3) as i:
                for u in range(2):
                    group(i * 2 + u, u, True, i)
            group(6, 0, True, 3)
            group(7, 1, False, 3)
            sp.wait_ge(out_stored, 16 + 32 * GROUPS)

        @block.gpsimd
        def _(pool):
            pool.dma_start(CONST[:], consts).then_inc(small_loaded, 16)
            pool.dma_start(WGT[:], wg).then_inc(small_loaded, 16)
            pool.dma_start(BG[:], bass.AP(bg.tensor, 0, [[0, 128], [1, E]])).then_inc(small_loaded, 16)
            regions = [(HOT[:], 0.0), (XN[:], 0.0), (WP[:], 0.0), (XG[0][TAPS * C:KC], 1.0)]
            for n, (region, value) in enumerate(regions):
                nc.gpsimd.memset(region, value).then_inc(pads_set, 1)
                pool.wait_ge(pads_set, n + 1)

            def features(g):
                pool.wait_ge(sums_ready, g + 1)
                pool.sem_inc(pool_go, 1)
                pool.dma_start(sums_dram, SUMS[:]).then_inc(sums_written, 16)
                pool.wait_ge(sums_written, g * 16 + 16)
                pool.sem_inc(pool_go, 1)
                pool.dma_start(FEAT[0:GN], sums_dram.rearrange("p k -> (p k)").rearrange("(n j) -> n j", j=C)
                               ).then_inc(feat_loaded, 16)

            def crop(g):
                pool.wait_ge(blocks_copied, g * LOTS + LOTS)
                pool.sem_inc(pool_go, 1)
                for b in range(GI):
                    nc.gpsimd.tensor_copy(KEPT[:, b].rearrange("p h (c v) -> p h c v", v=4),
                                          bass.AP(WY, b * NP * C, [[GI * NP * C, PIX], [1, 4], [NP, C], [NB, 4]])
                                          ).then_inc(kept_ready, 1)

            features(0)
            pool.wait_ge(parts_written, 16)
            nc.gpsimd.memset(XG[1][TAPS * C:KC], 1.0).then_inc(pads_set, 1)
            with pool.Fori(0, GROUPS - 1) as g:
                features(g + 1)
                crop(g)
            crop(GROUPS - 1)

        @block.vector
        def _(dve):
            steps = [0]

            def then_next(ins):
                steps[0] += 1
                ins.then_inc(chain, 1)
                dve.wait_ge(chain, steps[0])

            def restart_chain():
                dve.sem_clear(chain)
                steps[0] = 0

            then_next(nc.vector.memset(W0, 0.0))
            dve.wait_ge(w_loaded, 16)
            raw = WR.rearrange("p (c i k x) -> p c k i x", c=WG, i=C, k=TAPS)
            w0 = W0.rearrange("p (c x m) -> p c x m", c=WG, x=TAPS)
            for kx in range(TAPS):
                nc.vector.tensor_copy(w0[:, :, kx, 0:TAPS * C].rearrange("p c (k i) -> p c k i", k=TAPS),
                                      raw[:, :, :, :, kx])
            dve.wait_ge(bias_loaded, 16)
            then_next(nc.vector.tensor_copy(w0[:, :, 0, TAPS * C], BT[:]))
            then_next(nc.vector.tensor_copy(WPART[:, 0, :], W0))
            then_next(nc.vector.tensor_tensor(W0, W0, WPART[:, 0, :], ALU.subtract))
            then_next(nc.vector.tensor_copy(WPART[:, 1, :], W0))
            then_next(nc.vector.tensor_tensor(W0, W0, WPART[:, 1, :], ALU.subtract))
            nc.vector.tensor_copy(WPART[:, 2, :], W0).then_inc(parts_split, 1)

            dve.wait_ge(small_loaded, 16 * 3)
            nc.vector.tensor_copy(IDB[:], ident)

            for g in range(GROUPS):
                dve.wait_ge(x_loaded[g], 16)
                for h in range(2):
                    last = nc.vector.bn_stats(STATS[:, g, 6 * h:6 * h + 6], XALL[:, g, 512 * h:512 * (h + 1)])
            then_next(last)
            for g in range(GROUPS):
                last = nc.vector.bn_aggr(MV[:, g, :], STATS[:, g, :])
            then_next(last)
            nc.vector.tensor_scalar(VAR[:], MV[:, :, 1], 1e-5, None, ALU.add).then_inc(var_ready, 1)
            dve.wait_ge(root_ready, 1)
            then_next(nc.vector.reciprocal(RSTD[:], ROOT[:]))
            then_next(nc.vector.tensor_tensor(NEWT[:], RSTD[:], RSTD[:], ALU.mult))
            then_next(nc.vector.tensor_tensor(NEWT[:], NEWT[:], VAR[:], ALU.mult))
            then_next(nc.vector.tensor_scalar(NEWT[:], NEWT[:], -0.5, 1.5, ALU.mult, ALU.add))
            then_next(nc.vector.tensor_tensor(RSTD[:], RSTD[:], NEWT[:], ALU.mult))
            dve.wait_ge(pads_set, 2)
            restart_chain()

            def windows(g):
                dve.wait_ge(xc_loaded, g * 16 + 16)
                inside = bass.AP(XN, PITCH + 1, [[PITCH * PITCH, 128], [PITCH, H], [1, W]])
                nc.vector.tensor_scalar(inside, XC[:].rearrange("p (h w) -> p h w", w=W),
                                        MV[:, bass.ds(g, 1), 0], RSTD[:, bass.ds(g, 1)],
                                        ALU.subtract, ALU.mult).then_inc(normalised, 1)
                dve.wait_ge(normalised, g + 1)
                size = NB * WIN * WIN
                for vi in range(NB):
                    last = nc.vector.tensor_copy(
                        WY[:, vi * size:(vi + 1) * size].rearrange("p (h r s) -> p h r s", h=NB, r=WIN),
                        bass.AP(XN, vi * PS * PITCH, [[PITCH * PITCH, 128], [PS, NB], [PITCH, WIN], [1, WIN]]))
                last.then_inc(windows_ready, 1)
                dve.wait_ge(windows_ready, g + 1)
                nc.vector.tensor_reduce(SUMS[:], WY[:, 0:NB * size].rearrange("p (k w) -> p k w", k=NP),
                                        AX.X, ALU.add).then_inc(sums_ready, 1)

            def turn(g):
                dve.wait_ge(turned, g + 1)
                nc.vector.tensor_copy(FEATT[:], chunk_bank[0][0:C, 0:GN]).then_inc(feat_ready, 1)

            def routing(g):
                dve.wait_ge(logits_done, g + 1)
                then_next(nc.vector.scalar_tensor_tensor(LOGIT[0:GN], chunk_bank[0][0:GN, 128:128 + E],
                                                         1.0 / (WIN * WIN), BG[0:GN], ALU.mult, ALU.add))
                then_next(nc.vector.tensor_reduce(LMAX[0:GN], LOGIT[0:GN], AX.X, ALU.max))
                nc.vector.tensor_scalar(LMINUS[0:GN], LOGIT[0:GN], LMAX[0:GN], None,
                                        ALU.subtract).then_inc(centred, 1)
                dve.wait_ge(centred, g + 1)
                then_next(nc.vector.scalar_tensor_tensor(LCODE[0:GN], LMINUS[0:GN], 0.0,
                                                         CONST[0:GN, C_CODE:C_CODE + E], ALU.is_ge, ALU.mult))
                then_next(nc.vector.tensor_reduce(LPICK[0:GN], LCODE[0:GN], AX.X, ALU.min))
                nc.vector.tensor_scalar(HOT[0:GN], CONST[0:GN, C_CODE:C_CODE + 128], LPICK[0:GN], None, ALU.is_equal)
                dve.wait_ge(exp_done, g + 1)
                then_next(nc.vector.reciprocal(PROB[0:GN], LSUM[0:GN]))
                nc.vector.tensor_scalar(PSEL[0:GN], CONST[0:GN, C_PATCH:C_PATCH + NP], PROB[0:GN], None,
                                        ALU.mult).then_inc(onehot_ready, 1)

            def selection(g, u):
                dve.wait_ge(select_done, g + 1)
                nc.vector.tensor_copy(HOTT[:], chunk_bank[1][:, 0:GN])
                nc.vector.tensor_copy(PB[u][:], chunk_bank[1][:, 128:128 + NP]).then_inc(select_copied, 1)

            def weigh(g, u, lot):
                dve.wait_ge(conv_done, g * LOTS + lot + 1)
                prob = bass.AP(PB[u], lot * LOT, [[NP, 128], [1, LOT], [0, PIX]])
                nc.vector.scalar_tensor_tensor(Z[lot % 2][:],
                                               conv_bank[lot % 2][:, 0:LOT * PIX].rearrange("p (n s) -> p n s", s=PIX),
                                               0.0, prob, ALU.max, ALU.mult).then_inc(z_ready, 1)

            def residual(g, u, q, i):
                dve.wait_ge(residual_loaded[u], 16 * (i + 1))
                dve.wait_ge(channels_done, g * 2 + q + 1)
                cells = XR[u][:, 2 * q:2 * q + 2, :].rearrange("p b (r h s) -> p (b r) h s", h=4, s=PS)
                blocks = channels_bank[q][:].rearrange("p (h r s) -> p r h s", h=4, s=PS)
                nc.vector.tensor_tensor(cells, blocks, cells, ALU.add).then_inc(out_ready, 1)

            windows(0)
            turn(0)
            routing(0)
            selection(0, 0)
            dve.wait_ge(pads_set, 5)
            restart_chain()

            def group(g, u, has_next, i):
                if has_next:
                    windows(g + 1)
                weigh(g, u, 0)
                if has_next:
                    turn(g + 1)
                weigh(g, u, 1)
                if has_next:
                    routing(g + 1)
                    selection(g + 1, 1 - u)
                for lot in range(2, LOTS):
                    weigh(g, u, lot)
                for q in range(2):
                    residual(g, u, q, i)
                restart_chain()

            with dve.Fori(0, 3) as i:
                for u in range(2):
                    group(i * 2 + u, u, True, i)
            group(6, 0, True, 3)
            group(7, 1, False, 3)

        @block.scalar
        def _(act):
            act.wait_ge(var_ready, 1)
            nc.scalar.activation(ROOT[:], VAR[:], ACT.Sqrt).then_inc(root_ready, 1)

            def exponent(g):
                act.wait_ge(centred, g + 1)
                nc.scalar.activation(LEXP[0:GN], LMINUS[0:GN], ACT.Exp, accum_out=LSUM[0:GN]).then_inc(exp_done, 1)

            def chunk(g, u, c):
                t, n = CHUNKS[c]
                act.wait_ge(chunk_done, g * NCH + c + 1)
                nc.scalar.copy(bass.AP(WS[u], t, [[GN * NW, KC], [1, n], [NW, GN]]),
                               chunk_bank[c % 2][0:KC, 0:n * GN].rearrange("p (t n) -> p t n", n=GN)
                               ).then_inc(chunk_copied, 1)

            def blocks(g, lot):
                act.wait_ge(blocks_done, g * LOTS + lot + 1)
                nc.scalar.copy(Y[:, :, lot * LOT * C:(lot + 1) * LOT * C].rearrange("p b (n c) -> p n b c", c=C),
                               blocks_bank[0:PIX, 0:LOT * 128].rearrange("p (n b c) -> p n b c", n=LOT, b=GI)
                               ).then_inc(blocks_copied, 1)

            exponent(0)
            for c in range(NCH):
                chunk(0, 0, c)

            def group(g, u, has_next):
                if has_next:
                    act.wait_ge(windows_written, g * 16 + 32)
                for step in group_order(has_next):
                    if step[0] == "select":
                        exponent(g + 1)
                    elif step[0] == "chunk":
                        chunk(g + 1, 1 - u, step[1])
                    elif step[0] == "blocks":
                        blocks(g, step[1])

            with act.Fori(0, 3) as i:
                for u in range(2):
                    group(i * 2 + u, u, True)
            group(6, 0, True)
            group(7, 1, False)

        @block.tensor
        def _(pe):
            def turn(g):
                pe.wait_ge(feat_loaded, g * 16 + 16)
                nc.tensor.transpose(chunk_bank[0][0:C, 0:GN], FEAT[0:GN, :], CONST[0:GN, C_ID:C_ID + GN]
                                    ).then_inc(turned, 1)

            def logits(g):
                pe.wait_ge(feat_ready, g + 1)
                nc.tensor.matmul(chunk_bank[0][0:GN, 128:128 + E], FEATT[:], WGT[:],
                                 start=True, stop=True).then_inc(logits_done, 1)

            def select(g):
                pe.wait_ge(onehot_ready, g + 1)
                nc.tensor.matmul(chunk_bank[1][:, 0:GN], HOT[0:GN, :], IDB[0:GN, 0:GN], start=True, stop=True)
                nc.tensor.matmul(chunk_bank[1][:, 128:128 + NP], CONST[0:GN, C_OWN:C_OWN + 128],
                                 PSEL[0:GN], start=True, stop=True).then_inc(select_done, 1)

            def chunk(g, c):
                t, n = CHUNKS[c]
                if c < 2:
                    pe.wait_ge(select_copied, g + 1)
                else:
                    pe.wait_ge(chunk_copied, g * NCH + c - 1)
                for j in range(n):
                    kx, co = divmod(t + j, C)
                    last = nc.tensor.matmul(chunk_bank[c % 2][0:KC, j * GN:(j + 1) * GN],
                                            WP[:, co, kx, :], HOTT[:], start=True, stop=True)
                last.then_inc(chunk_done, 1)

            def conv(u, n):
                for kx in range(TAPS):
                    for b in range(GI):
                        patch = b * NP + n
                        o = conv_bank[n // LOT % 2][b * C:(b + 1) * C, n % LOT * PIX:(n % LOT + 1) * PIX]
                        taps = bass.AP(XG[u], patch * KROWS + kx, [[GN * KROWS, KC], [WIN, PS], [1, PS]])
                        last = nc.tensor.matmul(o, WS[u][0:KC, patch, kx * C:(kx + 1) * C], taps,
                                                start=kx == 0, stop=kx == TAPS - 1)
                return last

            def blocks(g, lot):
                pe.wait_ge(z_ready, g * LOTS + lot + 1)
                if lot:
                    pe.wait_ge(blocks_copied, g * LOTS + lot)
                pe.sem_inc(pe_go, 1)
                for j in range(LOT):
                    last = nc.tensor.transpose(blocks_bank[0:PIX, j * 128:(j + 1) * 128], Z[lot % 2][:, j, :], ident)
                last.then_inc(blocks_done, 1)

            def channels(g, q):
                for b in range(2):
                    pe.wait_ge(kept_ready, g * GI + 2 * q + b + 1)
                    pe.sem_inc(pe_go, 1)
                    for hi in range(4):
                        at = (hi * 2 + b) * PIX
                        last = nc.tensor.transpose(channels_bank[q][:, at:at + PIX], KEPT[:, 2 * q + b, hi],
                                                   CONST[0:PIX, C_ID:C_ID + PIX])
                last.then_inc(channels_done, 1)

            pe.wait_ge(small_loaded, 16 * 3)
            turn(0)
            logits(0)
            select(0)
            pe.wait_ge(wp_loaded, 16)
            for c in range(NCH):
                chunk(0, c)

            def group(g, u, has_next, i):
                pe.wait_ge(chunk_copied, (g + 1) * NCH)
                pe.wait_ge(xg_loaded[u], 16 * TAPS * (i + 1))
                for step in group_order(has_next):
                    if step[0] == "conv":
                        last = conv(u, step[1])
                        if step[1] % LOT == LOT - 1:
                            last.then_inc(conv_done, 1)
                    elif step[0] == "turn":
                        turn(g + 1)
                    elif step[0] == "logits":
                        logits(g + 1)
                    elif step[0] == "select":
                        select(g + 1)
                    elif step[0] == "chunk":
                        chunk(g + 1, step[1])
                    elif step[0] == "blocks":
                        blocks(g, step[1])
                    else:
                        channels(g, step[1])

            with pe.Fori(0, 3) as i:
                for u in range(2):
                    group(i * 2 + u, u, True, i)
            group(6, 0, True, 3)
            group(7, 1, False, 3)


def constants():
    import numpy as np

    c = np.zeros((128, C_END), np.float32)
    c[:, C_ID:C_ID + 128] = np.eye(128)
    for b in range(GI):
        for n in range(NP):
            c[b * NP + n, C_OWN + b * C:C_OWN + (b + 1) * C] = 1.0
            c[b * NP + n, C_PATCH + n] = 1.0
    c[:, C_CODE:C_CODE + 128] = 1.0
    for part in range(PARTS):
        c[:, C_CODE + part * E:C_CODE + (part + 1) * E] = np.arange(E) - E
    return c


def kernel(x, L0_conv_Wg, L0_conv_bg, L0_conv_Wexp, L0_conv_bexp):
    import numpy as np
    import concourse.bacc as bacc
    from concourse.bass_utils import run_bass_kernel_spmd

    nc = bacc.Bacc("TRN2", target_bir_lowering=False, num_devices=1)
    given = {"x": x, "wg": L0_conv_Wg, "bg": L0_conv_bg, "wexp": L0_conv_Wexp, "bexp": L0_conv_bexp}
    arrays = {name: np.ascontiguousarray(a) for name, a in given.items()}
    arrays["consts"] = constants()
    args = [nc.dram_tensor(name, a.shape, mybir.dt.from_np(a.dtype), kind="ExternalInput").ap()
            for name, a in arrays.items()]
    out = nc.dram_tensor("out", (B, C, H, W), mybir.dt.float32, kind="ExternalOutput").ap()
    build(nc, *args, out)
    result = run_bass_kernel_spmd(nc, [arrays], core_ids=[0])
    return result.results[0]["out"]
```

```python
from contextlib import ExitStack

import concourse.bass as bass
from concourse import mybir

B, C, H, W = 32, 32, 32, 32
E, TAPS, PS = 8, 3, 8
NB = 5
NP = NB * NB
GI, GROUPS = 4, B // 4
GN = GI * NP
PIX = PS * PS
WIN = PS + 2
PITCH = NB * PS + 2
KROWS = PS * WIN
KC = TAPS * C + 1
NW = TAPS * C
WG = C // 16
PARTS = 3
LOT, LOTS = NB, NP // NB
CH = 5
CHUNKS = [(t, min(CH, NW - t)) for t in range(0, NW, CH)]
WARM_UP = 2

C_ID, C_OWN, C_PATCH, C_CODE, C_END = 0, 128, 256, 256 + NP, 384 + NP


ROUTING_AT = {3: "turn", 4: "logits", 8: "select"}


def group_order(has_prev, has_next):
    chunks = [("chunk", c) for c in range(len(CHUNKS))] if has_next else []
    order = []
    for n in range(NP):
        order.append(("conv", n))
        if n in (1, 2, 3)[:3] or n > 9 and n % 2 and not has_next:
            order.append(("warm", 1))
        if has_next and n in ROUTING_AT:
            order.append((ROUTING_AT[n],))
        if n > max(ROUTING_AT) and len(chunks) > 3:
            order.append(chunks.pop(0))
            if n % 5 == 4:
                order.append(chunks.pop(0))
        if has_prev and n in (6, 7):
            order.append(("channels", n - 6))
        if n >= LOT and n % LOT == 4:
            order.append(("blocks", n // LOT - 1))
    order += chunks + [("warm", 1)]
    return order + [("blocks", LOTS - 1)]


def build(nc, x, wg, bg, wexp, bexp, consts, out):
    fp32, bf16 = mybir.dt.float32, mybir.dt.bfloat16
    ALU, ACT, AX = mybir.AluOpType, mybir.ActivationFunctionType, mybir.AxisListType

    with ExitStack() as ctx:
        def sb(name, shape, dt=fp32):
            return ctx.enter_context(nc.sbuf_tensor(name, shape, dt))

        def bank(name, banks=1):
            return ctx.enter_context(nc.psum_tensor(name, [128, 512 * banks], fp32))

        def sem(name):
            return ctx.enter_context(nc.semaphore(name))

        XG = [sb(f"XG{u}", [128, GN, KROWS]) for u in range(2)]
        WS = [sb(f"WS{u}", [128, GN, NW]) for u in range(2)]
        XR = [sb(f"XR{u}", [128, GI, 256]) for u in range(2)]
        XN = sb("XN", [128, PITCH * PITCH])
        WIND = sb("WIND", [128, NP * WIN * WIN])
        Y = sb("Y", [PIX, GI, NP * C])
        Z = [sb(f"Z{i}", [128, LOT, PIX]) for i in range(2)]
        KEPT = sb("KEPT", [64, GI, 4, C * 4])
        WPF = sb("WPF", [128, C * TAPS * KC], bf16)
        BT = sb("BT", [128, WG])
        CONST = sb("CONST", [128, C_END])
        IDB = sb("IDB", [128, 128], bf16)
        WGT = sb("WGT", [C, E])
        BG = sb("BG", [128, E])
        STATS = sb("STATS", [128, GROUPS, 12])
        MV = sb("MV", [128, GROUPS, 2])
        VAR, ROOT, RSTD, NEWT = (sb(n, [128, GROUPS]) for n in ("VAR", "ROOT", "RSTD", "NEWT"))
        SUMS = sb("SUMS", [128, NP])
        FEAT = [sb(f"FEAT{u}", [128, C]) for u in range(2)]
        FEATT = sb("FEATT", [C, GN])
        LOGIT, LMINUS, LEXP, LCODE = (sb(n, [128, E]) for n in ("LOGIT", "LMINUS", "LEXP", "LCODE"))
        LMAX, LSUM, LPICK, PROB = (sb(n, [128, 1]) for n in ("LMAX", "LSUM", "LPICK", "PROB"))
        HOT = sb("HOT", [128, 128], bf16)
        PSEL = sb("PSEL", [128, NP])
        HOTT = sb("HOTT", [128, GN], bf16)
        PB = [sb(f"PB{u}", [128, NP]) for u in range(2)]

        XALL = WS[1][:].rearrange("p n w -> p (n w)")[:, 0:GROUPS * H * W].rearrange("p (g f) -> p g f", g=GROUPS)
        XC = WIND[:, 0:H * W]
        WP = WPF[:].rearrange("p (c k m) -> p c k m", c=C, k=TAPS)
        ident = CONST[:, C_ID:C_ID + 128]

        WROW = WG * TAPS * KC
        spare = XG[1][:].rearrange("p n k -> p (n k)")
        WR = spare[:, 0:WG * C * 9]
        W0 = spare[:, 1024:1024 + WROW]
        WPART = spare[:, 2048:2048 + PARTS * WROW // 2].bitcast(bf16).rearrange("p (t f) -> p t f", t=PARTS)

        conv_bank = [bank(f"conv_bank{i}") for i in range(2)]
        chunk_bank = [bank(f"chunk_bank{i}") for i in range(2)]
        channels_bank = [bank(f"channels_bank{i}") for i in range(2)]
        blocks_bank = bank("blocks_bank", 2)
        FIRST_BANKS = chunk_bank + conv_bank

        parts_dram = nc.dram_tensor("weight_parts", (PARTS, 128, WROW), bf16).ap()
        windows_dram = [nc.dram_tensor(f"windows{u}", (GI * C * NP, WIN * WIN), fp32).ap() for u in range(2)]
        sums_dram = [nc.dram_tensor(f"sums{u}", (GI * C, NP), fp32).ap() for u in range(2)]

        x_loaded = [sem(f"x_loaded{g}") for g in range(GROUPS)]
        xc_loaded = sem("xc_loaded")
        w_loaded, bias_loaded, small_loaded = sem("w_loaded"), sem("bias_loaded"), sem("small_loaded")
        rest_ready, part_ready, parts_written, wp_loaded = sem("rest_ready"), sem("part_ready"), sem("parts_written"), sem("wp_loaded")
        pads_set, wp_zeroed, ones_set = sem("pads_set"), sem("wp_zeroed"), sem("ones_set")
        chain = sem("chain")
        var_ready, root_ready, normalised = sem("var_ready"), sem("root_ready"), sem("normalised")
        windows_ready, windows_written = sem("windows_ready"), sem("windows_written")
        sums_ready, sums_written, feat_loaded = sem("sums_ready"), sem("sums_written"), sem("feat_loaded")
        first_sums_written, first_feat_loaded = sem("first_sums_written"), sem("first_feat_loaded")
        sums_free, sums_turnable = sem("sums_free"), sem("sums_turnable")
        xg_loaded = [sem(f"xg_loaded{u}") for u in range(2)]
        residual_loaded = [sem(f"residual_loaded{u}") for u in range(2)]
        turned, feat_ready, logits_done = sem("turned"), sem("feat_ready"), sem("logits_done")
        centred, exp_done = sem("centred"), sem("exp_done")
        onehot_ready, select_done, select_copied = sem("onehot_ready"), sem("select_done"), sem("select_copied")
        chunk_done, chunk_copied = sem("chunk_done"), sem("chunk_copied")
        conv_done, z_ready = sem("conv_done"), sem("z_ready")
        blocks_done, blocks_copied = sem("blocks_done"), sem("blocks_copied")
        pool_go, pe_go, sp_go, kept_ready = sem("pool_go"), sem("pe_go"), sem("sp_go"), sem("kept_ready")
        channels_done, out_ready, out_stored = sem("channels_done"), sem("out_ready"), sem("out_stored")

        NCH = len(CHUNKS)
        x_rows = x.rearrange("(g b) c h w -> g (b c) (h w)", b=GI)
        x_rows_all = x.rearrange("b c h w -> (b c) (h w)")
        x_quarters = x.rearrange("b c (v r) w -> (c v) b (r w)", v=4)
        out_quarters = out.rearrange("b c (v r) w -> (c v) b (r w)", v=4)

        block = ctx.enter_context(nc.Block())

        @block.sync
        def _(sp):
            sp.dma_start(XALL[:, 0, :], x_rows[0]).then_inc(x_loaded[0], 16)
            sp.dma_start(WR, wexp.rearrange("e (g c) i h w -> (e g) (c i h w)", c=WG)).then_inc(w_loaded, 16)
            sp.dma_start(BT[:], bexp.rearrange("e (g c) -> (e g) c", c=WG)).then_inc(bias_loaded, 16)
            for g in range(1, 5):
                sp.dma_start(XALL[:, g, :], x_rows[g]).then_inc(x_loaded[g], 16)

            def write_windows(g, u):
                sp.wait_ge(windows_ready, g + 1)
                sp.dma_start(windows_dram[u].rearrange("(p k) w -> p (k w)", k=NP), WIND[:]
                             ).then_inc(windows_written, 16)

            def read_patches(u, first=0, end=TAPS):
                for ky in range(first, end):
                    sp.dma_start(XG[u][ky * C:(ky + 1) * C],
                                 windows_dram[u].rearrange("(n j) w -> j n w", j=C)[:, :, ky * WIN:ky * WIN + KROWS]
                                 ).then_inc(xg_loaded[u], 16)

            def quarters(g, u):
                sp.dma_start(XR[u][:], x_quarters[:, bass.ds(g * GI, GI), :]).then_inc(residual_loaded[u], 16)

            write_windows(0, 0)
            sp.wait_ge(sums_ready, 1)
            sp.dma_start(sums_dram[0], SUMS[:]).then_inc(first_sums_written, 16)
            sp.wait_ge(part_ready, PARTS)
            sp.dma_start(parts_dram.rearrange("t p f -> p t f"), WPART).then_inc(parts_written, 16)
            sp.wait_ge(first_sums_written, 16)
            sp.dma_start(FEAT[0][0:GN], sums_dram[0].rearrange("p k -> (p k)").rearrange("(n j) -> n j", j=C)
                         ).then_inc(first_feat_loaded, 16)
            sp.wait_ge(windows_written, 16)
            read_patches(0, 0, 1)
            sp.wait_ge(parts_written, 16)
            sp.wait_ge(wp_zeroed, 1)
            sp.dma_start(WPF[0:PARTS * E],
                         parts_dram.rearrange("t (e g) f -> (t e) (g f)", g=16)).then_inc(wp_loaded, 16)
            read_patches(0, 1, 2)
            sp.wait_ge(sums_ready, 2)
            sp.dma_start(sums_dram[1], SUMS[:]).then_inc(first_sums_written, 16)
            read_patches(0, 2, 3)
            sp.wait_ge(first_sums_written, 32)
            sp.dma_start(FEAT[1][0:GN], sums_dram[1].rearrange("p k -> (p k)").rearrange("(n j) -> n j", j=C)
                         ).then_inc(first_feat_loaded, 16)
            for g in range(5, GROUPS):
                sp.dma_start(XALL[:, g, :], x_rows[g]).then_inc(x_loaded[g], 16)
            quarters(0, 0)
            write_windows(1, 1)

            def stores(g, u):
                for q in range(2):
                    sp.wait_ge(out_ready, g * 2 + q + 1)
                    sp.dma_start(out_quarters[:, bass.ds(g * GI + 2 * q, 2), :],
                                 XR[u][:, 2 * q:2 * q + 2, :]).then_inc(out_stored, 16)

            def group(g, u, has_prev=True, has_next=True, has_second=True):
                if has_next:
                    sp.wait_ge(sums_ready, g + 2)
                    sp.sem_inc(sp_go, 1)
                    sp.wait_ge(windows_written, g * 16 + 32)
                if has_second:
                    sp.dma_start(XC, x_rows_all[bass.ds((g + 2) * GI * C, GI * C), :]).then_inc(xc_loaded, 16)
                if has_next and has_prev:
                    sp.wait_ge(conv_done, g * LOTS)
                    sp.sem_inc(sp_go, 1)
                if has_next:
                    read_patches(1 - u)
                if has_prev:
                    stores(g - 1, 1 - u)
                if has_second:
                    write_windows(g + 2, u)
                if has_next and has_prev:
                    sp.wait_ge(out_stored, g * 32)
                    sp.sem_inc(sp_go, 1)
                if has_next:
                    quarters(g + 1, 1 - u)

            group(0, 0, has_prev=False)
            with sp.Fori(0, 2) as i:
                for k in range(2):
                    group(i * 2 + (k + 1), 1 - k)
            group(5, 1)
            group(6, 0, has_second=False)
            group(7, 1, has_next=False, has_second=False)
            stores(7, 1)
            sp.wait_ge(out_stored, 32 * GROUPS)

        @block.gpsimd
        def _(pool):
            def split_weights():
                pool.wait_ge(pads_set, 1)
                pool.wait_ge(w_loaded, 16)
                raw = WR.rearrange("p (c i k x) -> p c k i x", c=WG, i=C, k=TAPS)
                w0 = W0.rearrange("p (c x m) -> p c x m", c=WG, x=TAPS)
                for kx in range(TAPS):
                    nc.gpsimd.tensor_copy(w0[:, :, kx, 0:TAPS * C].rearrange("p c (k i) -> p c k i", k=TAPS),
                                          raw[:, :, :, :, kx])
                pool.wait_ge(bias_loaded, 16)
                nc.gpsimd.tensor_copy(w0[:, :, 0, TAPS * C], BT[:]).then_inc(rest_ready, 1)
                for part in range(PARTS - 1):
                    pool.wait_ge(part_ready, part + 1)
                    nc.gpsimd.tensor_tensor(W0, W0, WPART[:, part, :], ALU.subtract).then_inc(rest_ready, 1)

            def send_sums(g, u):
                pool.wait_ge(sums_ready, g + 1)
                pool.sem_inc(pool_go, 1)
                pool.dma_start(sums_dram[u], SUMS[:]).then_inc(sums_written, 16)

            def fetch_sums(g, u):
                pool.wait_ge(sums_written, (g - 1) * 16)
                pool.sem_inc(sums_free, 1)
                pool.dma_start(FEAT[u][0:GN], sums_dram[u].rearrange("p k -> (p k)").rearrange("(n j) -> n j", j=C)
                               ).then_inc(feat_loaded, 16)

            def crop(g, lots):
                for lot in lots:
                    done = lot * LOT * C // NP
                    whole = (lot + 1) * LOT * C // NP
                    if lot == 0 and not (isinstance(g, int) and g == 0):
                        pool.wait_ge(channels_done, g * 2)
                        pool.sem_inc(pool_go, 1)
                    pool.wait_ge(blocks_copied, g * LOTS + lot + 1)
                    pool.sem_inc(pool_go, 1)
                    for b in range(GI):
                        kept = nc.gpsimd.tensor_copy(
                            bass.AP(KEPT, b * 16 * C + done * 4, [[GI * 16 * C, PIX], [4 * C, 4], [1, 4 * (whole - done)]]
                                    ).rearrange("p h (c v) -> p h c v", v=4),
                            bass.AP(Y, b * NP * C + done * NP,
                                    [[GI * NP * C, PIX], [1, 4], [NP, whole - done], [NB, 4]]))
                        if lot == LOTS - 1:
                            kept.then_inc(kept_ready, 1)

            nc.gpsimd.memset(WPF[:].bitcast(fp32), 0.0).then_inc(wp_zeroed, 1)
            pool.wait_ge(wp_zeroed, 1)
            split_weights()
            pool.wait_ge(rest_ready, PARTS)
            nc.gpsimd.memset(XG[0][TAPS * C:KC], 1.0).then_inc(ones_set, 1)
            pool.wait_ge(parts_written, 16)
            pool.wait_ge(ones_set, 1)
            nc.gpsimd.memset(XG[1][TAPS * C:KC], 1.0).then_inc(ones_set, 1)
            pool.wait_ge(ones_set, 2)
            def group(g, u):
                crop(g, range(0, 1))
                send_sums(g + 2, u)
                crop(g, range(1, 2))
                fetch_sums(g + 2, u)
                crop(g, range(2, LOTS))
                pool.wait_ge(feat_loaded, g * 16 + 16)
                pool.sem_inc(sums_turnable, 1)

            group(0, 0)
            with pool.Fori(0, 2) as i:
                for k in range(2):
                    group(i * 2 + (k + 1), 1 - k)
            group(5, 1)
            crop(6, range(LOTS))
            crop(7, range(LOTS))

        @block.vector
        def _(dve):
            steps = [0]

            def then_next(ins):
                steps[0] += 1
                ins.then_inc(chain, 1)
                dve.wait_ge(chain, steps[0])

            def restart_chain():
                dve.sem_clear(chain)
                steps[0] = 0

            def statistics(first, end, turn):
                for g in range(first, end):
                    dve.wait_ge(x_loaded[g], 16)
                    for h in range(2):
                        last = nc.vector.bn_stats(STATS[:, g, 6 * h:6 * h + 6], XALL[:, g, 512 * h:512 * (h + 1)])
                then_next(last)
                for g in range(first, end):
                    last = nc.vector.bn_aggr(MV[:, g, :], STATS[:, g, :])
                then_next(last)
                r, t, v = (a[:, first:end] for a in (RSTD, NEWT, VAR))
                nc.vector.tensor_scalar(v, MV[:, first:end, 1], 1e-5, None, ALU.add).then_inc(var_ready, 1)
                dve.wait_ge(root_ready, turn)
                then_next(nc.vector.reciprocal(r, ROOT[:, first:end]))
                then_next(nc.vector.tensor_tensor(t, r, r, ALU.mult))
                then_next(nc.vector.tensor_tensor(t, t, v, ALU.mult))
                then_next(nc.vector.tensor_scalar(t, t, -0.5, 1.5, ALU.mult, ALU.add))
                then_next(nc.vector.tensor_tensor(r, r, t, ALU.mult))

            def normalise(g, rows):
                inside = bass.AP(XN, PITCH + 1, [[PITCH * PITCH, 128], [PITCH, H], [1, W]])
                nc.vector.tensor_scalar(inside, rows.rearrange("p (h w) -> p h w", w=W),
                                        MV[:, bass.ds(g, 1), 0], RSTD[:, bass.ds(g, 1)],
                                        ALU.subtract, ALU.mult).then_inc(normalised, 1)
                dve.wait_ge(normalised, g + 1)

            def windows(g, first, end):
                size = NB * WIN * WIN
                for vi in range(first, end):
                    last = nc.vector.tensor_copy(
                        WIND[:, vi * size:(vi + 1) * size].rearrange("p (h r s) -> p h r s", h=NB, r=WIN),
                        bass.AP(XN, vi * PS * PITCH, [[PITCH * PITCH, 128], [PS, NB], [PITCH, WIN], [1, WIN]]))
                if end == NB:
                    last.then_inc(windows_ready, 1)

            def sums(g):
                dve.wait_ge(windows_ready, g + 1)
                nc.vector.tensor_reduce(SUMS[:], WIND[:].rearrange("p (k w) -> p k w", k=NP),
                                        AX.X, ALU.add).then_inc(sums_ready, 1)

            def turn(g):
                dve.wait_ge(turned, g + 1)
                nc.vector.tensor_copy(FEATT[:], chunk_bank[0][0:C, 0:GN]).then_inc(feat_ready, 1)

            def routing(g):
                dve.wait_ge(logits_done, g + 1)
                then_next(nc.vector.scalar_tensor_tensor(LOGIT[0:GN], chunk_bank[0][0:GN, 128:128 + E],
                                                         1.0 / (WIN * WIN), BG[0:GN], ALU.mult, ALU.add))
                then_next(nc.vector.tensor_reduce(LMAX[0:GN], LOGIT[0:GN], AX.X, ALU.max))
                nc.vector.tensor_scalar(LMINUS[0:GN], LOGIT[0:GN], LMAX[0:GN], None,
                                        ALU.subtract).then_inc(centred, 1)
                dve.wait_ge(centred, g + 1)
                then_next(nc.vector.scalar_tensor_tensor(LCODE[0:GN], LMINUS[0:GN], 0.0,
                                                         CONST[0:GN, C_CODE:C_CODE + E], ALU.is_ge, ALU.mult))
                then_next(nc.vector.tensor_reduce(LPICK[0:GN], LCODE[0:GN], AX.X, ALU.min))
                nc.vector.tensor_scalar(HOT[0:GN], CONST[0:GN, C_CODE:C_CODE + 128], LPICK[0:GN], None, ALU.is_equal)
                dve.wait_ge(exp_done, g + 1)
                then_next(nc.vector.reciprocal(PROB[0:GN], LSUM[0:GN]))
                nc.vector.tensor_scalar(PSEL[0:GN], CONST[0:GN, C_PATCH:C_PATCH + NP], PROB[0:GN], None,
                                        ALU.mult).then_inc(onehot_ready, 1)

            def selection(g, u):
                dve.wait_ge(select_done, g + 1)
                nc.vector.tensor_copy(HOTT[:], chunk_bank[1][:, 0:GN])
                nc.vector.tensor_copy(PB[u][:], chunk_bank[1][:, 128:128 + NP]).then_inc(select_copied, 1)

            def weigh(g, u, lot):
                dve.wait_ge(conv_done, g * LOTS + lot + 1)
                prob = bass.AP(PB[u], lot * LOT, [[NP, 128], [1, LOT], [0, PIX]])
                nc.vector.scalar_tensor_tensor(Z[lot % 2][:],
                                               conv_bank[lot % 2][:, 0:LOT * PIX].rearrange("p (n s) -> p n s", s=PIX),
                                               0.0, prob, ALU.max, ALU.mult).then_inc(z_ready, 1)

            def residual(g, u, q, i):
                dve.wait_ge(residual_loaded[u], 16 * (i + 1))
                dve.wait_ge(channels_done, g * 2 + q + 1)
                cells = XR[u][:, 2 * q:2 * q + 2, :].rearrange("p b (r h s) -> p (b r) h s", h=4, s=PS)
                blocks = channels_bank[q][:].rearrange("p (h r s) -> p r h s", h=4, s=PS)
                nc.vector.tensor_tensor(cells, blocks, cells, ALU.add).then_inc(out_ready, 1)

            for region in (W0, XN[:], HOT[:]):
                nc.vector.memset(region, 0.0).then_inc(pads_set, 1)
            statistics(0, 1, 1)
            dve.wait_ge(pads_set, 3)
            normalise(0, XALL[:, 0, :])
            windows(0, 0, NB)
            sums(0)
            dve.wait_ge(small_loaded, 16 * 3)
            nc.vector.tensor_copy(IDB[:], ident)
            statistics(1, 2, 2)
            turn(0)
            routing(0)
            selection(0, 0)
            dve.wait_ge(windows_written, 16)
            normalise(1, XALL[:, 1, :])
            windows(1, 0, NB)
            dve.wait_ge(first_sums_written, 16)
            sums(1)
            dve.wait_ge(first_sums_written, 32)
            dve.sem_inc(sums_free, 1)
            statistics(2, GROUPS, 3)
            restart_chain()

            def group(g, u, i, has_prev=True, has_next=True, has_second=True):
                if has_next:
                    turn(g + 1)
                    routing(g + 1)
                if has_prev:
                    for q in range(2):
                        residual(g - 1, 1 - u, q, i if u else i - 1)
                weigh(g, u, 0)
                if has_next:
                    selection(g + 1, 1 - u)
                if has_second:
                    dve.wait_ge(xc_loaded, g * 16 + 16)
                    normalise(g + 2, XC)
                weigh(g, u, 1)
                if has_second:
                    windows(g + 2, 0, NB)
                    dve.wait_ge(sums_free, g + 1)
                    sums(g + 2)
                weigh(g, u, 2)
                for lot in range(3, LOTS):
                    weigh(g, u, lot)
                restart_chain()

            group(0, 0, 0, has_prev=False)
            with dve.Fori(0, 2) as i:
                for k in range(2):
                    group(i * 2 + (k + 1), 1 - k, i + k)
            group(5, 1, 2)
            group(6, 0, 3, has_second=False)
            group(7, 1, 3, has_next=False, has_second=False)
            for q in range(2):
                residual(7, 1, q, 3)

        @block.scalar
        def _(act):
            def root(first, end, turn):
                act.wait_ge(var_ready, turn)
                nc.scalar.activation(ROOT[:, first:end], VAR[:, first:end], ACT.Sqrt).then_inc(root_ready, 1)

            def exponent(g):
                act.wait_ge(centred, g + 1)
                nc.scalar.activation(LEXP[0:GN], LMINUS[0:GN], ACT.Exp, accum_out=LSUM[0:GN]).then_inc(exp_done, 1)

            def chunk(g, u, c, banks=chunk_bank):
                t, n = CHUNKS[c]
                act.wait_ge(chunk_done, g * NCH + c + 1)
                nc.scalar.copy(bass.AP(WS[u], t, [[GN * NW, KC], [1, n], [NW, GN]]),
                               banks[c % len(banks)][0:KC, 0:n * GN].rearrange("p (t n) -> p t n", n=GN)
                               ).then_inc(chunk_copied, 1)

            def blocks(g, lot):
                act.wait_ge(blocks_done, g * LOTS + lot + 1)
                nc.scalar.copy(Y[:, :, lot * LOT * C:(lot + 1) * LOT * C].rearrange("p b (n c) -> p n b c", c=C),
                               blocks_bank[0:PIX, 0:LOT * 128].rearrange("p (n b c) -> p n b c", n=LOT, b=GI)
                               ).then_inc(blocks_copied, 1)

            act.dma_start(CONST[:], consts).then_inc(small_loaded, 16)
            act.dma_start(WGT[:], wg).then_inc(small_loaded, 16)
            act.dma_start(BG[:], bass.AP(bg.tensor, 0, [[0, 128], [1, E]])).then_inc(small_loaded, 16)
            root(0, 1, 1)
            for part in range(PARTS):
                act.wait_ge(rest_ready, part + 1)
                nc.scalar.copy(WPART[:, part, :], W0).then_inc(part_ready, 1)
            root(1, 2, 2)
            exponent(0)
            for c in range(NCH):
                chunk(0, 0, c, FIRST_BANKS)
            root(2, GROUPS, 3)

            def group(g, u, has_prev=True, has_next=True):
                for step in group_order(has_prev, has_next):
                    if step[0] == "logits":
                        exponent(g + 1)
                    elif step[0] == "chunk":
                        chunk(g + 1, 1 - u, step[1])
                    elif step[0] == "blocks":
                        blocks(g, step[1])

            group(0, 0, has_prev=False)
            with act.Fori(0, 2) as i:
                for k in range(2):
                    group(i * 2 + (k + 1), 1 - k)
            group(5, 1)
            group(6, 0)
            group(7, 1, has_next=False)

        @block.tensor
        def _(pe):
            def turn(g, u):
                nc.tensor.transpose(chunk_bank[0][0:C, 0:GN], FEAT[u][0:GN, :], CONST[0:GN, C_ID:C_ID + GN]
                                    ).then_inc(turned, 1)

            def logits(g):
                pe.wait_ge(feat_ready, g + 1)
                nc.tensor.matmul(chunk_bank[0][0:GN, 128:128 + E], FEATT[:], WGT[:],
                                 start=True, stop=True).then_inc(logits_done, 1)

            def select(g):
                pe.wait_ge(onehot_ready, g + 1)
                nc.tensor.matmul(chunk_bank[1][:, 0:GN], HOT[0:GN, :], IDB[0:GN, 0:GN], start=True, stop=True)
                nc.tensor.matmul(chunk_bank[1][:, 128:128 + NP], CONST[0:GN, C_OWN:C_OWN + 128],
                                 PSEL[0:GN], start=True, stop=True).then_inc(select_done, 1)

            def chunk(g, c, banks=chunk_bank):
                t, n = CHUNKS[c]
                if c < len(banks):
                    pe.wait_ge(select_copied, g + 1)
                else:
                    pe.wait_ge(chunk_copied, g * NCH + c + 1 - len(banks))
                for j in range(n):
                    kx, co = divmod(t + j, C)
                    last = nc.tensor.matmul(banks[c % len(banks)][0:KC, j * GN:(j + 1) * GN],
                                            WP[:, co, kx, :], HOTT[:], start=True, stop=True)
                last.then_inc(chunk_done, 1)

            def conv(u, n):
                for kx in range(TAPS):
                    for b in range(GI):
                        patch = b * NP + n
                        o = conv_bank[n // LOT % 2][b * C:(b + 1) * C, n % LOT * PIX:(n % LOT + 1) * PIX]
                        taps = bass.AP(XG[u], patch * KROWS + kx, [[GN * KROWS, KC], [WIN, PS], [1, PS]])
                        last = nc.tensor.matmul(o, WS[u][0:KC, patch, kx * C:(kx + 1) * C], taps,
                                                start=kx == 0, stop=kx == TAPS - 1)
                return last

            def blocks(g, lot):
                pe.wait_ge(z_ready, g * LOTS + lot + 1)
                if lot:
                    pe.wait_ge(blocks_copied, g * LOTS + lot)
                pe.sem_inc(pe_go, 1)
                for j in range(LOT):
                    last = nc.tensor.transpose(blocks_bank[0:PIX, j * 128:(j + 1) * 128], Z[lot % 2][:, j, :], ident)
                last.then_inc(blocks_done, 1)

            def channels(g, q):
                for b in range(2):
                    pe.wait_ge(kept_ready, g * GI + 2 * q + b + 1)
                    pe.sem_inc(pe_go, 1)
                    for hi in range(4):
                        at = (hi * 2 + b) * PIX
                        last = nc.tensor.transpose(channels_bank[q][:, at:at + PIX], KEPT[:, 2 * q + b, hi],
                                                   CONST[0:PIX, C_ID:C_ID + PIX])
                last.then_inc(channels_done, 1)

            pe.wait_ge(small_loaded, 16 * 3)
            pe.wait_ge(first_feat_loaded, 16)
            turn(0, 0)
            logits(0)
            select(0)
            pe.wait_ge(wp_loaded, 16)
            for c in range(NCH):
                chunk(0, c, FIRST_BANKS)

            pe.wait_ge(first_feat_loaded, 32)
            pe.sem_inc(sums_turnable, 1)

            def warm_up(wide, bank):
                for _ in range(wide):
                    nc.tensor.matmul(bank[:], IDB[:], WPF[:, 0:512], start=True, stop=True)

            def group(g, u, i, has_prev=True, has_next=True):
                pe.wait_ge(chunk_copied, (g + 1) * NCH)
                pe.wait_ge(xg_loaded[u], 16 * TAPS * (i + 1))
                pe.wait_ge(ones_set, u + 1)
                warm_up(WARM_UP, conv_bank[1])
                at = 0
                for step in group_order(has_prev, has_next):
                    if step[0] == "conv":
                        at = step[1]
                        last = conv(u, at)
                        if step[1] % LOT == LOT - 1:
                            last.then_inc(conv_done, 1)
                    elif step[0] == "warm":
                        warm_up(step[1], conv_bank[1] if at < LOT - 1 else channels_bank[1])
                    elif step[0] == "turn":
                        pe.wait_ge(sums_turnable, g + 1)
                        turn(g + 1, 1 - u)
                    elif step[0] == "logits":
                        logits(g + 1)
                    elif step[0] == "select":
                        select(g + 1)
                    elif step[0] == "chunk":
                        chunk(g + 1, step[1])
                    elif step[0] == "blocks":
                        blocks(g, step[1])
                    else:
                        channels(g - 1, step[1])

            group(0, 0, 0, has_prev=False)
            with pe.Fori(0, 2) as i:
                for k in range(2):
                    group(i * 2 + (k + 1), 1 - k, i + k)
            group(5, 1, 2)
            group(6, 0, 3)
            group(7, 1, 3, has_next=False)
            for q in range(2):
                channels(7, q)


def constants():
    import numpy as np

    c = np.zeros((128, C_END), np.float32)
    c[:, C_ID:C_ID + 128] = np.eye(128)
    for b in range(GI):
        for n in range(NP):
            c[b * NP + n, C_OWN + b * C:C_OWN + (b + 1) * C] = 1.0
            c[b * NP + n, C_PATCH + n] = 1.0
    c[:, C_CODE:C_CODE + 128] = 1.0
    for part in range(PARTS):
        c[:, C_CODE + part * E:C_CODE + (part + 1) * E] = np.arange(E) - E
    return c


def kernel(x, L0_conv_Wg, L0_conv_bg, L0_conv_Wexp, L0_conv_bexp):
    import numpy as np
    import concourse.bacc as bacc
    from concourse.bass_utils import run_bass_kernel_spmd

    nc = bacc.Bacc("TRN2", target_bir_lowering=False, num_devices=1)
    given = {"x": x, "wg": L0_conv_Wg, "bg": L0_conv_bg, "wexp": L0_conv_Wexp, "bexp": L0_conv_bexp}
    arrays = {name: np.ascontiguousarray(a) for name, a in given.items()}
    arrays["consts"] = constants()
    args = [nc.dram_tensor(name, a.shape, mybir.dt.from_np(a.dtype), kind="ExternalInput").ap()
            for name, a in arrays.items()]
    out = nc.dram_tensor("out", (B, C, H, W), mybir.dt.float32, kind="ExternalOutput").ap()
    build(nc, *args, out)
    result = run_bass_kernel_spmd(nc, [arrays], core_ids=[0])
    return result.results[0]["out"]
```

```python
from contextlib import ExitStack

import concourse.bass as bass
from concourse import mybir

B, C, H, W = 32, 32, 32, 32
E, TAPS, PS = 8, 3, 8
NB = 5
NP = NB * NB
GI, GROUPS = 4, B // 4
GN = GI * NP
PIX = PS * PS
WIN = PS + 2
PITCH = NB * PS + 2
KROWS = PS * WIN
KC = TAPS * C + 1
NW = TAPS * C
WG = C // 16
PARTS = 3
LOT, LOTS = NB, NP // NB
CH = 5
CHUNKS = [(t, min(CH, NW - t)) for t in range(0, NW, CH)]

C_ID, C_OWN, C_PATCH, C_CODE, C_END = 0, 128, 256, 256 + NP, 384 + NP

LAST_BLOCKS_AT = 1
ROUTING_AT = {2: "turn", 3: "logits", 6: "select"}
CHANNELS_AT = {7: 0, 8: 1}
CHUNKS_AT = (7, 9, 11, 13, 14, 16, 18, 20, 22, 23)
EARLY = 2
LATE_AT = {4: 2, 6: 3, 8: 4}
WARM_AT, FIRST_WARM_AT, LAST_WARM_AT = (2, 3, 4), (5, 6, 7, 8), (16, 18, 20, 22)
WARM_UP = 4


def group_order(has_prev, has_next):
    chunks = [("chunk", c) for c in range(len(CHUNKS))] if has_next else []
    order = []
    for n in range(NP):
        order.append(("conv", n))
        if has_prev and n == LAST_BLOCKS_AT:
            order.append(("last blocks",))
        if n in ROUTING_AT and has_next:
            order.append((ROUTING_AT[n],))
        if n in WARM_AT or not has_prev and n in FIRST_WARM_AT or not has_next and n in LAST_WARM_AT:
            order.append(("warm", n))
        if has_prev and n in CHANNELS_AT:
            order.append(("channels", CHANNELS_AT[n]))
        if n in CHUNKS_AT:
            order += chunks[:2]
            chunks = chunks[2:]
        if n >= LOT and n % LOT == 4:
            order.append(("blocks", n // LOT - 1))
    return order + chunks


def build(nc, x, wg, bg, wexp, bexp, consts, out):
    fp32, bf16 = mybir.dt.float32, mybir.dt.bfloat16
    ALU, ACT, AX = mybir.AluOpType, mybir.ActivationFunctionType, mybir.AxisListType

    with ExitStack() as ctx:
        def sb(name, shape, dt=fp32):
            return ctx.enter_context(nc.sbuf_tensor(name, shape, dt))

        def bank(name, banks=1):
            return ctx.enter_context(nc.psum_tensor(name, [128, 512 * banks], fp32))

        def sem(name):
            return ctx.enter_context(nc.semaphore(name))

        XG = [sb(f"XG{u}", [128, GN, KROWS]) for u in range(2)]
        WS = [sb(f"WS{u}", [128, GN, NW]) for u in range(2)]
        XR = [sb(f"XR{u}", [128, GI, 256]) for u in range(2)]
        XN = sb("XN", [128, PITCH * PITCH])
        WIND = sb("WIND", [128, NP * WIN * WIN])
        Y = sb("Y", [PIX, GI, NP * C])
        Z = [sb(f"Z{i}", [128, LOT, PIX]) for i in range(2)]
        KEPT = sb("KEPT", [64, GI, 4, C * 4])
        WPF = sb("WPF", [128, C * TAPS * KC], bf16)
        BT = sb("BT", [128, WG])
        CONST = sb("CONST", [128, C_END])
        IDB = sb("IDB", [128, 128], bf16)
        WGT = sb("WGT", [C, E])
        BG = sb("BG", [128, E])
        STATS = sb("STATS", [128, 12])
        MV = sb("MV", [128, 2])
        VAR, LN, ROOT, RSTD, NEWT = (sb(n, [128, 1]) for n in ("VAR", "LN", "ROOT", "RSTD", "NEWT"))
        SUMS = sb("SUMS", [128, NP])
        FEAT = [sb(f"FEAT{u}", [128, C]) for u in range(2)]
        FEATT = sb("FEATT", [C, GN])
        LOGIT, LMINUS, LEXP, LCODE = (sb(n, [128, E]) for n in ("LOGIT", "LMINUS", "LEXP", "LCODE"))
        LMAX, LSUM, LPICK, PROB = (sb(n, [128, 1]) for n in ("LMAX", "LSUM", "LPICK", "PROB"))
        HOT = sb("HOT", [128, 128], bf16)
        PSEL = sb("PSEL", [128, NP])
        HOTT = sb("HOTT", [128, GN], bf16)
        PB = [sb(f"PB{u}", [128, NP]) for u in range(2)]

        XALL = WS[1][:].rearrange("p n w -> p (n w)")[:, 0:3 * H * W].rearrange("p (g f) -> p g f", g=3)
        XC = WIND[:, 0:H * W]
        WP = WPF[:].rearrange("p (c k m) -> p c k m", c=C, k=TAPS)
        ident = CONST[:, C_ID:C_ID + 128]

        WROW = WG * TAPS * KC
        spare = XG[1][:].rearrange("p n k -> p (n k)")
        WR = spare[:, 0:WG * C * 9]
        W0 = spare[:, 1024:1024 + WROW]
        WPART = spare[:, 2048:2048 + PARTS * WROW // 2].bitcast(bf16).rearrange("p (t f) -> p t f", t=PARTS)

        conv_bank = [bank(f"conv_bank{i}") for i in range(2)]
        chunk_bank = [bank(f"chunk_bank{i}") for i in range(2)]
        channels_bank = [bank(f"channels_bank{i}") for i in range(2)]
        blocks_bank = bank("blocks_bank", 2)
        FIRST_BANKS = chunk_bank + conv_bank

        parts_dram = nc.dram_tensor("weight_parts", (PARTS, 128, WROW), bf16).ap()
        windows_dram = [nc.dram_tensor(f"windows{u}", (GI * C * NP, WIN * WIN), fp32).ap() for u in range(2)]
        sums_dram = [nc.dram_tensor(f"sums{u}", (GI * C, NP), fp32).ap() for u in range(2)]

        x_loaded = [sem(f"x_loaded{g}") for g in range(3)]
        xc_loaded = sem("xc_loaded")
        w_loaded, bias_loaded, small_loaded = sem("w_loaded"), sem("bias_loaded"), sem("small_loaded")
        rest_ready, part_ready = sem("rest_ready"), sem("part_ready")
        parts_written, wp_loaded = sem("parts_written"), sem("wp_loaded")
        pads_set, wp_zeroed, ones_set = sem("pads_set"), sem("wp_zeroed"), sem("ones_set")
        chain = sem("chain")
        var_ready, ln_done, root_ready = sem("var_ready"), sem("ln_done"), sem("root_ready")
        normalised = sem("normalised")
        windows_ready, windows_written = sem("windows_ready"), sem("windows_written")
        sums_ready, sums_written, feat_loaded = sem("sums_ready"), sem("sums_written"), sem("feat_loaded")
        first_sums_written, first_feat_loaded = sem("first_sums_written"), sem("first_feat_loaded")
        sums_free, sums_turnable = sem("sums_free"), sem("sums_turnable")
        early_filled, late_filled = sem("early_filled"), sem("late_filled")
        first_tap_loaded = [sem(f"first_tap_loaded{u}") for u in range(2)]
        last_tap_loaded = [sem(f"last_tap_loaded{u}") for u in range(2)]
        residual_loaded = [sem(f"residual_loaded{u}") for u in range(2)]
        turned, feat_ready, logits_done = sem("turned"), sem("feat_ready"), sem("logits_done")
        centred, exp_done = sem("centred"), sem("exp_done")
        onehot_ready, select_done, select_copied = sem("onehot_ready"), sem("select_done"), sem("select_copied")
        chunk_done, chunk_copied = sem("chunk_done"), sem("chunk_copied")
        conv_done, z_ready = sem("conv_done"), sem("z_ready")
        blocks_done, blocks_copied = sem("blocks_done"), sem("blocks_copied")
        pool_go, pe_go, sp_go, kept_ready = sem("pool_go"), sem("pe_go"), sem("sp_go"), sem("kept_ready")
        channels_done, out_ready, out_stored = sem("channels_done"), sem("out_ready"), sem("out_stored")

        NCH = len(CHUNKS)
        x_rows = x.rearrange("(g b) c h w -> g (b c) (h w)", b=GI)
        x_rows_all = x.rearrange("b c h w -> (b c) (h w)")
        x_quarters = x.rearrange("b c (v r) w -> (c v) b (r w)", v=4)
        out_quarters = out.rearrange("b c (v r) w -> (c v) b (r w)", v=4)

        def middle_tap(u, lot):
            first, middle, third = (XG[u][ky * C:(ky + 1) * C].rearrange("p (b n) k -> p b n k", b=GI)
                                    [:, :, lot * LOT:(lot + 1) * LOT] for ky in range(TAPS))
            return [(middle[:, :, :, 0:KROWS - WIN], first[:, :, :, WIN:KROWS]),
                    (middle[:, :, :, KROWS - WIN:KROWS], third[:, :, :, KROWS - 2 * WIN:KROWS - WIN])]

        block = ctx.enter_context(nc.Block())

        @block.sync
        def _(sp):
            sp.dma_start(XALL[:, 0, :], x_rows[0]).then_inc(x_loaded[0], 16)
            sp.dma_start(WR, wexp.rearrange("e (g c) i h w -> (e g) (c i h w)", c=WG)).then_inc(w_loaded, 16)
            sp.dma_start(BT[:], bexp.rearrange("e (g c) -> (e g) c", c=WG)).then_inc(bias_loaded, 16)
            for g in range(1, 3):
                sp.dma_start(XALL[:, g, :], x_rows[g]).then_inc(x_loaded[g], 16)

            def write_windows(g, u):
                sp.wait_ge(windows_ready, g + 1)
                sp.dma_start(windows_dram[u].rearrange("(p k) w -> p (k w)", k=NP), WIND[:]
                             ).then_inc(windows_written, 16)

            def read_patches(u):
                for ky, loaded in (0, first_tap_loaded[u]), (2, last_tap_loaded[u]):
                    sp.dma_start(XG[u][ky * C:(ky + 1) * C],
                                 windows_dram[u].rearrange("(n j) w -> j n w", j=C)[:, :, ky * WIN:ky * WIN + KROWS]
                                 ).then_inc(loaded, 16)

            def quarters(g, u):
                sp.dma_start(XR[u][:], x_quarters[:, bass.ds(g * GI, GI), :]).then_inc(residual_loaded[u], 16)

            write_windows(0, 0)
            sp.wait_ge(sums_ready, 1)
            sp.dma_start(sums_dram[0], SUMS[:]).then_inc(first_sums_written, 16)
            sp.wait_ge(part_ready, PARTS)
            sp.dma_start(parts_dram.rearrange("t p f -> p t f"), WPART).then_inc(parts_written, 16)
            sp.wait_ge(first_sums_written, 16)
            sp.dma_start(FEAT[0][0:GN], sums_dram[0].rearrange("p k -> (p k)").rearrange("(n j) -> n j", j=C)
                         ).then_inc(first_feat_loaded, 16)
            sp.wait_ge(parts_written, 16)
            sp.wait_ge(wp_zeroed, 1)
            sp.dma_start(WPF[0:PARTS * E],
                         parts_dram.rearrange("t (e g) f -> (t e) (g f)", g=16)).then_inc(wp_loaded, 16)
            sp.wait_ge(windows_written, 16)
            read_patches(0)
            sp.wait_ge(sums_ready, 2)
            sp.dma_start(sums_dram[1], SUMS[:]).then_inc(first_sums_written, 16)
            sp.wait_ge(first_sums_written, 32)
            sp.dma_start(FEAT[1][0:GN], sums_dram[1].rearrange("p k -> (p k)").rearrange("(n j) -> n j", j=C)
                         ).then_inc(first_feat_loaded, 16)
            write_windows(1, 1)
            quarters(0, 0)

            def stores(g, u):
                for q in range(2):
                    sp.wait_ge(out_ready, g * 2 + q + 1)
                    sp.dma_start(out_quarters[:, bass.ds(g * GI + 2 * q, 2), :],
                                 XR[u][:, 2 * q:2 * q + 2, :]).then_inc(out_stored, 16)

            def group(g, u, has_prev=True, has_next=True, has_second=True):
                if has_next:
                    sp.wait_ge(sums_ready, g + 2)
                    sp.sem_inc(sp_go, 1)
                    sp.wait_ge(windows_written, g * 16 + 32)
                if has_prev and has_second:
                    sp.dma_start(XC, x_rows_all[bass.ds((g + 2) * GI * C, GI * C), :]).then_inc(xc_loaded, 16)
                if has_next and has_prev:
                    sp.wait_ge(conv_done, g * LOTS)
                    sp.sem_inc(sp_go, 1)
                    sp.wait_ge(sums_turnable, g + 1)
                    sp.sem_inc(sp_go, 1)
                if has_next:
                    read_patches(1 - u)
                if has_prev:
                    stores(g - 1, 1 - u)
                if has_second:
                    write_windows(g + 2, u)
                if has_next and has_prev:
                    sp.wait_ge(out_stored, g * 32)
                    sp.sem_inc(sp_go, 1)
                if has_next:
                    quarters(g + 1, 1 - u)

            group(0, 0, has_prev=False)
            with sp.Fori(0, 2) as i:
                for k in range(2):
                    group(i * 2 + (k + 1), 1 - k)
            group(5, 1)
            group(6, 0, has_second=False)
            group(7, 1, has_next=False, has_second=False)
            stores(7, 1)
            sp.wait_ge(out_stored, 32 * GROUPS)

        @block.gpsimd
        def _(pool):
            def split_weights():
                pool.wait_ge(pads_set, 1)
                pool.wait_ge(w_loaded, 16)
                raw = WR.rearrange("p (c i k x) -> p c k i x", c=WG, i=C, k=TAPS)
                w0 = W0.rearrange("p (c x m) -> p c x m", c=WG, x=TAPS)
                for kx in range(TAPS):
                    nc.gpsimd.tensor_copy(w0[:, :, kx, 0:TAPS * C].rearrange("p c (k i) -> p c k i", k=TAPS),
                                          raw[:, :, :, :, kx])
                pool.wait_ge(bias_loaded, 16)
                nc.gpsimd.tensor_copy(w0[:, :, 0, TAPS * C], BT[:]).then_inc(rest_ready, 1)
                for part in range(PARTS - 1):
                    pool.wait_ge(part_ready, part + 1)
                    nc.gpsimd.tensor_tensor(W0, W0, WPART[:, part, :], ALU.subtract).then_inc(rest_ready, 1)

            def send_sums(g, u):
                pool.wait_ge(sums_ready, g + 1)
                pool.sem_inc(pool_go, 1)
                pool.dma_start(sums_dram[u], SUMS[:]).then_inc(sums_written, 16)

            def fetch_sums(g, u):
                pool.wait_ge(sums_written, (g - 1) * 16)
                pool.sem_inc(sums_free, 1)
                pool.dma_start(FEAT[u][0:GN], sums_dram[u].rearrange("p k -> (p k)").rearrange("(n j) -> n j", j=C)
                               ).then_inc(feat_loaded, 16)

            def crop(g, lots):
                for lot in lots:
                    done = lot * LOT * C // NP
                    whole = (lot + 1) * LOT * C // NP
                    if lot == 0 and not (isinstance(g, int) and g == 0):
                        pool.wait_ge(channels_done, g * 2)
                        pool.sem_inc(pool_go, 1)
                    pool.wait_ge(blocks_copied, g * LOTS + lot + 1)
                    pool.sem_inc(pool_go, 1)
                    for b in range(GI):
                        kept = nc.gpsimd.tensor_copy(
                            bass.AP(KEPT, b * 16 * C + done * 4, [[GI * 16 * C, PIX], [4 * C, 4], [1, 4 * (whole - done)]]
                                    ).rearrange("p h (c v) -> p h c v", v=4),
                            bass.AP(Y, b * NP * C + done * NP,
                                    [[GI * NP * C, PIX], [1, 4], [NP, whole - done], [NB, 4]]))
                        if lot == LOTS - 1:
                            kept.then_inc(kept_ready, 1)

            nc.gpsimd.memset(WPF[:].bitcast(fp32), 0.0).then_inc(wp_zeroed, 1)
            pool.wait_ge(wp_zeroed, 1)
            split_weights()
            pool.wait_ge(rest_ready, PARTS)
            nc.gpsimd.memset(XG[0][TAPS * C:KC], 1.0).then_inc(ones_set, 1)
            pool.wait_ge(parts_written, 16)
            pool.wait_ge(ones_set, 1)
            nc.gpsimd.memset(XG[1][TAPS * C:KC], 1.0).then_inc(ones_set, 1)
            pool.wait_ge(ones_set, 2)

            def group(g, u):
                crop(g, range(0, 1))
                send_sums(g + 2, u)
                crop(g, range(1, 2))
                fetch_sums(g + 2, u)
                crop(g, range(2, LOTS - 1))
                pool.wait_ge(feat_loaded, g * 16 + 16)
                pool.sem_inc(sums_turnable, 1)
                crop(g, range(LOTS - 1, LOTS))

            group(0, 0)
            with pool.Fori(0, 2) as i:
                for k in range(2):
                    group(i * 2 + (k + 1), 1 - k)
            group(5, 1)
            crop(6, range(LOTS))
            crop(7, range(LOTS))

        @block.vector
        def _(dve):
            steps = [0]

            def then_next(ins):
                steps[0] += 1
                ins.then_inc(chain, 1)
                dve.wait_ge(chain, steps[0])

            def restart_chain():
                dve.sem_clear(chain)
                steps[0] = 0

            def statistics(g, rows):
                for h in range(2):
                    last = nc.vector.bn_stats(STATS[:, 6 * h:6 * h + 6], rows[:, 512 * h:512 * (h + 1)])
                then_next(last)
                then_next(nc.vector.bn_aggr(MV[:], STATS[:]))
                nc.vector.tensor_scalar(VAR[:], MV[:, 1:2], 1e-5, None, ALU.add).then_inc(var_ready, 1)

            def deviation(g):
                dve.wait_ge(root_ready, g + 1)
                then_next(nc.vector.tensor_tensor(NEWT[:], ROOT[:], ROOT[:], ALU.mult))
                then_next(nc.vector.tensor_tensor(NEWT[:], NEWT[:], VAR[:], ALU.mult))
                then_next(nc.vector.tensor_scalar(NEWT[:], NEWT[:], -0.5, 1.5, ALU.mult, ALU.add))
                then_next(nc.vector.tensor_tensor(RSTD[:], ROOT[:], NEWT[:], ALU.mult))

            def normalise(g, rows):
                inside = bass.AP(XN, PITCH + 1, [[PITCH * PITCH, 128], [PITCH, H], [1, W]])
                nc.vector.tensor_scalar(inside, rows.rearrange("p (h w) -> p h w", w=W),
                                        MV[:, 0:1], RSTD[:],
                                        ALU.subtract, ALU.mult).then_inc(normalised, 1)
                dve.wait_ge(normalised, g + 1)

            def windows():
                size = NB * WIN * WIN
                for vi in range(NB):
                    last = nc.vector.tensor_copy(
                        WIND[:, vi * size:(vi + 1) * size].rearrange("p (h r s) -> p h r s", h=NB, r=WIN),
                        bass.AP(XN, vi * PS * PITCH, [[PITCH * PITCH, 128], [PS, NB], [PITCH, WIN], [1, WIN]]))
                last.then_inc(windows_ready, 1)

            def sums(g):
                dve.wait_ge(windows_ready, g + 1)
                nc.vector.tensor_reduce(SUMS[:], WIND[:].rearrange("p (k w) -> p k w", k=NP),
                                        AX.X, ALU.add).then_inc(sums_ready, 1)

            def turn(g):
                dve.wait_ge(turned, g + 1)
                nc.vector.tensor_copy(FEATT[:], chunk_bank[0][0:C, 0:GN]).then_inc(feat_ready, 1)

            def routing(g):
                dve.wait_ge(logits_done, g + 1)
                then_next(nc.vector.scalar_tensor_tensor(LOGIT[0:GN], chunk_bank[0][0:GN, 128:128 + E],
                                                         1.0 / (WIN * WIN), BG[0:GN], ALU.mult, ALU.add))
                then_next(nc.vector.tensor_reduce(LMAX[0:GN], LOGIT[0:GN], AX.X, ALU.max))
                nc.vector.tensor_scalar(LMINUS[0:GN], LOGIT[0:GN], LMAX[0:GN], None,
                                        ALU.subtract).then_inc(centred, 1)
                dve.wait_ge(centred, g + 1)
                then_next(nc.vector.scalar_tensor_tensor(LCODE[0:GN], LMINUS[0:GN], 0.0,
                                                         CONST[0:GN, C_CODE:C_CODE + E], ALU.is_ge, ALU.mult))
                then_next(nc.vector.tensor_reduce(LPICK[0:GN], LCODE[0:GN], AX.X, ALU.min))
                nc.vector.tensor_scalar(HOT[0:GN], CONST[0:GN, C_CODE:C_CODE + 128], LPICK[0:GN], None, ALU.is_equal)
                dve.wait_ge(exp_done, g + 1)
                then_next(nc.vector.reciprocal(PROB[0:GN], LSUM[0:GN]))
                nc.vector.tensor_scalar(PSEL[0:GN], CONST[0:GN, C_PATCH:C_PATCH + NP], PROB[0:GN], None,
                                        ALU.mult).then_inc(onehot_ready, 1)

            def selection(g, u):
                dve.wait_ge(select_done, g + 1)
                nc.vector.tensor_copy(HOTT[:], chunk_bank[1][:, 0:GN])
                nc.vector.tensor_copy(PB[u][:], chunk_bank[1][:, 128:128 + NP]).then_inc(select_copied, 1)

            def early_lots(u, turn):
                for part, loaded in enumerate((first_tap_loaded[u], last_tap_loaded[u])):
                    dve.wait_ge(loaded, 16 * turn)
                    for lot in range(EARLY):
                        to, source = middle_tap(u, lot)[part]
                        last = nc.vector.tensor_copy(to, source)
                last.then_inc(early_filled, 1)

            def weigh(g, u, lot):
                dve.wait_ge(conv_done, g * LOTS + lot + 1)
                prob = bass.AP(PB[u], lot * LOT, [[NP, 128], [1, LOT], [0, PIX]])
                nc.vector.scalar_tensor_tensor(Z[(lot + u) % 2][:],
                                               conv_bank[(lot + u) % 2][:, 0:LOT * PIX].rearrange("p (n s) -> p n s", s=PIX),
                                               0.0, prob, ALU.max, ALU.mult).then_inc(z_ready, 1)

            def residual(g, u, q, i):
                dve.wait_ge(residual_loaded[u], 16 * (i + 1))
                dve.wait_ge(channels_done, g * 2 + q + 1)
                cells = XR[u][:, 2 * q:2 * q + 2, :].rearrange("p b (r h s) -> p (b r) h s", h=4, s=PS)
                blocks = channels_bank[q][:].rearrange("p (h r s) -> p r h s", h=4, s=PS)
                nc.vector.tensor_tensor(cells, blocks, cells, ALU.add).then_inc(out_ready, 1)

            for region in (W0, XN[:], HOT[:]):
                nc.vector.memset(region, 0.0).then_inc(pads_set, 1)
            dve.wait_ge(x_loaded[0], 16)
            statistics(0, XALL[:, 0, :])
            deviation(0)
            dve.wait_ge(pads_set, 3)
            normalise(0, XALL[:, 0, :])
            windows()
            sums(0)
            dve.wait_ge(small_loaded, 16 * 3)
            nc.vector.tensor_copy(IDB[:], ident)
            dve.wait_ge(x_loaded[1], 16)
            statistics(1, XALL[:, 1, :])
            deviation(1)
            turn(0)
            routing(0)
            selection(0, 0)
            dve.wait_ge(windows_written, 16)
            normalise(1, XALL[:, 1, :])
            windows()
            dve.wait_ge(first_sums_written, 16)
            sums(1)
            dve.wait_ge(x_loaded[2], 16)
            statistics(2, XALL[:, 2, :])
            early_lots(0, 1)
            dve.wait_ge(first_sums_written, 32)
            dve.sem_inc(sums_free, 1)
            restart_chain()

            def group(g, u, i, has_prev=True, has_next=True, has_second=True):
                if has_prev and has_second:
                    dve.wait_ge(xc_loaded, g * 16)
                    statistics(g + 2, XC)
                if has_next:
                    turn(g + 1)
                    routing(g + 1)
                if not has_prev:
                    deviation(2)
                    normalise(2, XALL[:, 2, :])
                if has_next:
                    selection(g + 1, 1 - u)
                weigh(g, u, 0)
                if has_prev:
                    for q in range(2):
                        residual(g - 1, 1 - u, q, i if u else i - 1)
                if has_prev and has_second:
                    deviation(g + 2)
                    normalise(g + 2, XC)
                if not has_prev:
                    dve.wait_ge(windows_written, 32)
                if has_second:
                    windows()
                weigh(g, u, 1)
                if has_second:
                    dve.wait_ge(sums_free, g + 1)
                    sums(g + 2)
                weigh(g, u, 2)
                weigh(g, u, 3)
                if has_next:
                    early_lots(1 - u, i + (1 + u))
                weigh(g, u, 4)
                restart_chain()

            group(0, 0, 0, has_prev=False)
            with dve.Fori(0, 2) as i:
                for k in range(2):
                    group(i * 2 + (k + 1), 1 - k, i + k)
            group(5, 1, 2)
            group(6, 0, 3, has_second=False)
            group(7, 1, 3, has_next=False, has_second=False)
            for q in range(2):
                residual(7, 1, q, 3)

        @block.scalar
        def _(act):
            def root(g):
                act.wait_ge(var_ready, g + 1)
                nc.scalar.activation(LN[:], VAR[:], ACT.Ln).then_inc(ln_done, 1)
                act.wait_ge(ln_done, g + 1)
                nc.scalar.activation(ROOT[:], LN[:], ACT.Exp, scale=-0.5).then_inc(root_ready, 1)

            def exponent(g):
                act.wait_ge(centred, g + 1)
                nc.scalar.activation(LEXP[0:GN], LMINUS[0:GN], ACT.Exp, accum_out=LSUM[0:GN]).then_inc(exp_done, 1)

            def chunk(g, u, c, banks=chunk_bank):
                t, n = CHUNKS[c]
                act.wait_ge(chunk_done, g * NCH + c + 1)
                nc.scalar.copy(bass.AP(WS[u], t, [[GN * NW, KC], [1, n], [NW, GN]]),
                               banks[c % len(banks)][0:KC, 0:n * GN].rearrange("p (t n) -> p t n", n=GN)
                               ).then_inc(chunk_copied, 1)

            def blocks(g, lot):
                act.wait_ge(blocks_done, g * LOTS + lot + 1)
                nc.scalar.copy(Y[:, :, lot * LOT * C:(lot + 1) * LOT * C].rearrange("p b (n c) -> p n b c", c=C),
                               blocks_bank[0:PIX, 0:LOT * 128].rearrange("p (n b c) -> p n b c", n=LOT, b=GI)
                               ).then_inc(blocks_copied, 1)

            act.dma_start(CONST[:], consts).then_inc(small_loaded, 16)
            act.dma_start(WGT[:], wg).then_inc(small_loaded, 16)
            act.dma_start(BG[:], bass.AP(bg.tensor, 0, [[0, 128], [1, E]])).then_inc(small_loaded, 16)
            root(0)
            for part in range(PARTS):
                act.wait_ge(rest_ready, part + 1)
                nc.scalar.copy(WPART[:, part, :], W0).then_inc(part_ready, 1)
            root(1)
            exponent(0)
            for c in range(NCH):
                chunk(0, 0, c, FIRST_BANKS)
            root(2)

            def late_lot(u, lot):
                for to, source in middle_tap(u, lot):
                    last = nc.scalar.copy(to, source)
                last.then_inc(late_filled, 1)

            def group(g, u, i, has_prev=True, has_next=True, has_second=True):
                act.wait_ge(first_tap_loaded[u], 16 * (i + 1))
                act.wait_ge(last_tap_loaded[u], 16 * (i + 1))
                for step in group_order(has_prev, has_next):
                    if step[0] == "logits":
                        exponent(g + 1)
                    elif step == ("conv", 1) and has_prev and has_second:
                        root(g + 2)
                    elif step[0] == "conv" and step[1] in LATE_AT:
                        late_lot(u, LATE_AT[step[1]])
                    elif step[0] == "chunk":
                        chunk(g + 1, 1 - u, step[1])
                    elif step[0] == "blocks":
                        blocks(g, step[1])
                    elif step[0] == "last blocks":
                        blocks(g - 1, LOTS - 1)

            group(0, 0, 0, has_prev=False)
            with act.Fori(0, 2) as i:
                for k in range(2):
                    group(i * 2 + (k + 1), 1 - k, i + k)
            group(5, 1, 2)
            group(6, 0, 3, has_second=False)
            group(7, 1, 3, has_next=False, has_second=False)
            blocks(7, LOTS - 1)

        @block.tensor
        def _(pe):
            def turn(g, u):
                nc.tensor.transpose(chunk_bank[0][0:C, 0:GN], FEAT[u][0:GN, :], CONST[0:GN, C_ID:C_ID + GN]
                                    ).then_inc(turned, 1)

            def logits(g):
                pe.wait_ge(feat_ready, g + 1)
                nc.tensor.matmul(chunk_bank[0][0:GN, 128:128 + E], FEATT[:], WGT[:],
                                 start=True, stop=True).then_inc(logits_done, 1)

            def select(g):
                pe.wait_ge(onehot_ready, g + 1)
                nc.tensor.matmul(chunk_bank[1][:, 0:GN], HOT[0:GN, :], IDB[0:GN, 0:GN], start=True, stop=True)
                nc.tensor.matmul(chunk_bank[1][:, 128:128 + NP], CONST[0:GN, C_OWN:C_OWN + 128],
                                 PSEL[0:GN], start=True, stop=True).then_inc(select_done, 1)

            def chunk(g, c, banks=chunk_bank):
                t, n = CHUNKS[c]
                if c < len(banks):
                    pe.wait_ge(select_copied, g + 1)
                else:
                    pe.wait_ge(chunk_copied, g * NCH + c + 1 - len(banks))
                for j in range(n):
                    kx, co = divmod(t + j, C)
                    last = nc.tensor.matmul(banks[c % len(banks)][0:KC, j * GN:(j + 1) * GN],
                                            WP[:, co, kx, :], HOTT[:], start=True, stop=True)
                last.then_inc(chunk_done, 1)

            def conv(u, n):
                for kx in range(TAPS):
                    for b in range(GI):
                        patch = b * NP + n
                        o = conv_bank[(n // LOT + u) % 2][b * C:(b + 1) * C, n % LOT * PIX:(n % LOT + 1) * PIX]
                        taps = bass.AP(XG[u], patch * KROWS + kx, [[GN * KROWS, KC], [WIN, PS], [1, PS]])
                        last = nc.tensor.matmul(o, WS[u][0:KC, patch, kx * C:(kx + 1) * C], taps,
                                                start=kx == 0, stop=kx == TAPS - 1)
                return last

            def blocks(g, u, lot):
                pe.wait_ge(z_ready, g * LOTS + lot + 1)
                if lot:
                    pe.wait_ge(blocks_copied, g * LOTS + lot)
                pe.sem_inc(pe_go, 1)
                for j in range(LOT):
                    last = nc.tensor.transpose(blocks_bank[0:PIX, j * 128:(j + 1) * 128],
                                               Z[(lot + u) % 2][:, j, :], ident)
                last.then_inc(blocks_done, 1)

            def channels(g, q):
                for b in range(2):
                    pe.wait_ge(kept_ready, g * GI + 2 * q + b + 1)
                    pe.sem_inc(pe_go, 1)
                    for hi in range(4):
                        at = (hi * 2 + b) * PIX
                        last = nc.tensor.transpose(channels_bank[q][:, at:at + PIX], KEPT[:, 2 * q + b, hi],
                                                   CONST[0:PIX, C_ID:C_ID + PIX])
                last.then_inc(channels_done, 1)

            pe.wait_ge(small_loaded, 16 * 3)
            pe.wait_ge(first_feat_loaded, 16)
            turn(0, 0)
            logits(0)
            select(0)

            def warm_up(wide, bank):
                for _ in range(wide):
                    nc.tensor.matmul(bank[:], IDB[:], WPF[:, 0:512], start=True, stop=True)

            pe.wait_ge(wp_loaded, 16)
            for c in range(NCH):
                chunk(0, c, FIRST_BANKS)
                warm_up(1, channels_bank[0])
            warm_up(WARM_UP, channels_bank[0])

            def group(g, u, i, has_prev=True, has_next=True):
                pe.wait_ge(chunk_copied, (g + 1) * NCH)
                pe.wait_ge(early_filled, g + 1)
                pe.wait_ge(ones_set, u + 1)
                for step in group_order(has_prev, has_next):
                    if step[0] == "conv":
                        at = step[1]
                        if at % LOT == 0 and at >= EARLY * LOT:
                            pe.wait_ge(late_filled, g * (LOTS - EARLY) + (at // LOT - EARLY + 1))
                        last = conv(u, at)
                        if at % LOT == LOT - 1:
                            last.then_inc(conv_done, 1)
                    elif step[0] == "warm":
                        warm_up(1, conv_bank[(1 + u) % 2] if step[1] < LOT else channels_bank[0])
                    elif step[0] == "turn":
                        if isinstance(g, int) and g == 0:
                            pe.wait_ge(first_feat_loaded, 32)
                            pe.sem_inc(sums_turnable, 1)
                        pe.wait_ge(sums_turnable, g + 1)
                        turn(g + 1, 1 - u)
                    elif step[0] == "logits":
                        logits(g + 1)
                    elif step[0] == "select":
                        select(g + 1)
                    elif step[0] == "chunk":
                        chunk(g + 1, step[1])
                    elif step[0] == "blocks":
                        blocks(g, u, step[1])
                    elif step[0] == "last blocks":
                        blocks(g - 1, 1 - u, LOTS - 1)
                    else:
                        channels(g - 1, step[1])

            group(0, 0, 0, has_prev=False)
            with pe.Fori(0, 2) as i:
                for k in range(2):
                    group(i * 2 + (k + 1), 1 - k, i + k)
            group(5, 1, 2)
            group(6, 0, 3)
            group(7, 1, 3, has_next=False)
            blocks(7, 1, LOTS - 1)
            for q in range(2):
                channels(7, q)


def constants():
    import numpy as np

    c = np.zeros((128, C_END), np.float32)
    c[:, C_ID:C_ID + 128] = np.eye(128)
    for b in range(GI):
        for n in range(NP):
            c[b * NP + n, C_OWN + b * C:C_OWN + (b + 1) * C] = 1.0
            c[b * NP + n, C_PATCH + n] = 1.0
    c[:, C_CODE:C_CODE + 128] = 1.0
    for part in range(PARTS):
        c[:, C_CODE + part * E:C_CODE + (part + 1) * E] = np.arange(E) - E
    return c


def kernel(x, L0_conv_Wg, L0_conv_bg, L0_conv_Wexp, L0_conv_bexp):
    import numpy as np
    import concourse.bacc as bacc
    from concourse.bass_utils import run_bass_kernel_spmd

    nc = bacc.Bacc("TRN2", target_bir_lowering=False, num_devices=1)
    given = {"x": x, "wg": L0_conv_Wg, "bg": L0_conv_bg, "wexp": L0_conv_Wexp, "bexp": L0_conv_bexp}
    arrays = {name: np.ascontiguousarray(a) for name, a in given.items()}
    arrays["consts"] = constants()
    args = [nc.dram_tensor(name, a.shape, mybir.dt.from_np(a.dtype), kind="ExternalInput").ap()
            for name, a in arrays.items()]
    out = nc.dram_tensor("out", (B, C, H, W), mybir.dt.float32, kind="ExternalOutput").ap()
    build(nc, *args, out)
    result = run_bass_kernel_spmd(nc, [arrays], core_ids=[0])
    return result.results[0]["out"]
```
